# Optimizing a Trainium2 kernel written in Bass

```python
import numpy as np
import jax
import jax.numpy as jnp

def _softmax(x, axis=-1):
    return jax.nn.softmax(x, axis=axis)

def _gelu(x):
    return jax.nn.gelu(x, approximate=True)

def _silu(x):
    return jax.nn.silu(x)

def _sigmoid(x):
    return jax.nn.sigmoid(x)

def _layernorm(x, axis=-1, eps=1e-05):
    m = jnp.mean(x, axis=axis, keepdims=True)
    v = jnp.var(x, axis=axis, keepdims=True)
    return (x - m) / jnp.sqrt(v + eps)

def _scatter_add(tgt, idx, src, axis=0):
    return tgt.at[idx].add(src)

def _segment_sum(src, seg, n):
    return jax.ops.segment_sum(src, seg, n)
kernel_name = 'mk_recurrent_d2_jaxref_r8_54255e'

def setup_inputs(seed: int=0):
    np.random.seed(seed)
    _w = jnp.asarray

    def _L0_attn_setup():
        import jax, jax.numpy as jnp
        import numpy as np
        B, T, D = (4, 256, 128)
        key = jax.random.key(seed)
        kx, kq, kk, kv = jax.random.split(key, 4)
        scale = 1.0 / np.sqrt(D)
        return {'x': jax.random.normal(kx, (B, T, D), dtype=jnp.float32), 'Wq': jax.random.normal(kq, (D, D), dtype=jnp.float32) * scale, 'Wk': jax.random.normal(kk, (D, D), dtype=jnp.float32) * scale, 'Wv': jax.random.normal(kv, (D, D), dtype=jnp.float32) * scale}
    _L0_attn_in = _L0_attn_setup()

    def _L0_ffn_setup():
        import jax, jax.numpy as jnp
        import numpy as np
        DIM = 128
        NUM_EXPERTS = 8
        TOP_K = 2
        key = jax.random.key(seed)
        ks = jax.random.split(key, 7)
        s_in = 1.0 / np.sqrt(DIM)
        s_hid = 1.0 / np.sqrt(4 * DIM)
        x = jax.random.normal(ks[0], (2, 256, DIM), dtype=jnp.float32)
        gate_w = jax.random.normal(ks[1], (DIM, NUM_EXPERTS), dtype=jnp.float32) * s_in
        gate_b = jax.random.normal(ks[2], (NUM_EXPERTS,), dtype=jnp.float32) * 0.01
        w1 = jax.random.normal(ks[3], (NUM_EXPERTS, DIM, 4 * DIM), dtype=jnp.float32) * s_in
        b1 = jax.random.normal(ks[4], (NUM_EXPERTS, 4 * DIM), dtype=jnp.float32) * 0.01
        w2 = jax.random.normal(ks[5], (NUM_EXPERTS, 4 * DIM, DIM), dtype=jnp.float32) * s_hid
        b2 = jax.random.normal(ks[6], (NUM_EXPERTS, DIM), dtype=jnp.float32) * 0.01
        return {'x': x, 'gate_w': gate_w, 'gate_b': gate_b, 'w1': w1, 'b1': b1, 'w2': w2, 'b2': b2}
    _L0_ffn_in = _L0_ffn_setup()

    def _L1_attn_setup():
        import jax, jax.numpy as jnp
        import numpy as np
        NUM_HEADS = 16
        EPS = 1e-06
        L2_EPS = 1e-12

        def _l2_normalize(x):
            n = jnp.linalg.norm(x, axis=-1, keepdims=True)
            return x / jnp.maximum(n, L2_EPS)
        key = jax.random.key(seed)
        k1, k2 = jax.random.split(key)
        x = jax.random.normal(k1, (2, 1024, 128), dtype=jnp.float32)
        W_qkv = jax.random.normal(k2, (384, 128), dtype=jnp.float32) * 0.02
        return {'x': x, 'W_qkv': W_qkv}
    _L1_attn_in = _L1_attn_setup()

    def _L1_ffn_setup():
        import jax, jax.numpy as jnp
        import numpy as np
        D_MODEL = 128
        D_FF = 512
        N_EXPERTS = 8
        INIT_SCALE = 0.1

        def _trunc_normal(key, shape, std):
            return std * jax.random.truncated_normal(key, -2.0, 2.0, shape, dtype=jnp.float32)
        key = jax.random.key(seed)
        ks = jax.random.split(key, 5)
        x = jax.random.normal(ks[0], (4, 128, D_MODEL), dtype=jnp.float32)
        router_W = _trunc_normal(ks[1], (D_MODEL, N_EXPERTS), INIT_SCALE / np.sqrt(D_MODEL))
        router_b = jnp.zeros((N_EXPERTS,), dtype=jnp.float32)
        W1 = _trunc_normal(ks[2], (N_EXPERTS, D_MODEL, D_FF), INIT_SCALE / np.sqrt(D_MODEL))
        b1 = jnp.zeros((N_EXPERTS, D_FF), dtype=jnp.float32)
        W2 = _trunc_normal(ks[3], (N_EXPERTS, D_FF, D_MODEL), INIT_SCALE / np.sqrt(D_FF))
        b2 = jnp.zeros((N_EXPERTS, D_MODEL), dtype=jnp.float32)
        return {'x': x, 'router_W': router_W, 'router_b': router_b, 'W1': W1, 'b1': b1, 'W2': W2, 'b2': b2}
    _L1_ffn_in = _L1_ffn_setup()
    _d = {'L0_attn_x': _L0_attn_in['x'], 'L0_attn_Wq': _L0_attn_in['Wq'], 'L0_attn_Wk': _L0_attn_in['Wk'], 'L0_attn_Wv': _L0_attn_in['Wv'], 'L0_ffn_gate_w': _L0_ffn_in['gate_w'], 'L0_ffn_gate_b': _L0_ffn_in['gate_b'], 'L0_ffn_w1': _L0_ffn_in['w1'], 'L0_ffn_b1': _L0_ffn_in['b1'], 'L0_ffn_w2': _L0_ffn_in['w2'], 'L0_ffn_b2': _L0_ffn_in['b2'], 'L1_attn_W_qkv': _L1_attn_in['W_qkv'], 'L1_ffn_router_W': _L1_ffn_in['router_W'], 'L1_ffn_router_b': _L1_ffn_in['router_b'], 'L1_ffn_W1': _L1_ffn_in['W1'], 'L1_ffn_b1': _L1_ffn_in['b1'], 'L1_ffn_W2': _L1_ffn_in['W2'], 'L1_ffn_b2': _L1_ffn_in['b2']}
    _x0 = _d['L0_attn_x']
    _d['L0_attn_x'] = jax.random.normal(jax.random.fold_in(jax.random.key(seed), 1), (16, 512, 128), dtype=_x0.dtype)
    del _x0
    return _d

def reference(L0_attn_x, L0_attn_Wq, L0_attn_Wk, L0_attn_Wv, L0_ffn_gate_w, L0_ffn_gate_b, L0_ffn_w1, L0_ffn_b1, L0_ffn_w2, L0_ffn_b2, L1_attn_W_qkv, L1_ffn_router_W, L1_ffn_router_b, L1_ffn_W1, L1_ffn_b1, L1_ffn_W2, L1_ffn_b2):

    def _L0_attn_ref(x, Wq, Wk, Wv):
        import jax, jax.numpy as jnp
        import numpy as np
        B, T, D = (4, 256, 128)
        q = jnp.einsum('btd,od->bto', x, Wq)
        k = jnp.einsum('btd,od->bto', x, Wk)
        v = jnp.einsum('btd,od->bto', x, Wv)
        scores = jnp.einsum('bqd,bkd->bqk', q, k)
        inv_sqrt_d = 1.0 / np.sqrt(k.shape[-1]).astype(np.float32)
        weights = jax.nn.softmax(scores * inv_sqrt_d, axis=-1)
        return jnp.einsum('bqk,bkd->bqd', weights, v)

    def _L0_ffn_ref(x, gate_w, gate_b, w1, b1, w2, b2):
        import jax, jax.numpy as jnp
        import numpy as np
        DIM = 128
        NUM_EXPERTS = 8
        TOP_K = 2
        B, N, C = x.shape
        flat_x = x.reshape(-1, C)
        logits = flat_x @ gate_w + gate_b
        _, topk_idx = jax.lax.top_k(logits, TOP_K)
        e_star = jnp.max(topk_idx, axis=-1)
        out = jnp.zeros_like(flat_x)
        for i in range(NUM_EXPERTS):
            h = jax.nn.gelu(flat_x @ w1[i] + b1[i], approximate=False)
            y = h @ w2[i] + b2[i]
            out = jnp.where((e_star == i)[:, None], y, out)
        return (TOP_K * out).reshape(B, N, C)

    def _L1_attn_ref(x, W_qkv):
        import jax, jax.numpy as jnp
        import numpy as np
        NUM_HEADS = 16
        EPS = 1e-06
        L2_EPS = 1e-12

        def _l2_normalize(x):
            n = jnp.linalg.norm(x, axis=-1, keepdims=True)
            return x / jnp.maximum(n, L2_EPS)
        b, n, dim = x.shape
        h = NUM_HEADS
        d = dim // h
        scale = d ** (-0.5)
        qkv = x @ W_qkv.T
        q, k, v = jnp.split(qkv, 3, axis=-1)
        to_heads = lambda t: t.reshape(b, n, h, d).transpose(0, 2, 1, 3)
        q, k, v = (to_heads(q), to_heads(k), to_heads(v))
        q = jax.nn.softplus(_l2_normalize(q))
        k = jax.nn.softplus(_l2_normalize(k))
        kv = jnp.einsum('bhnd,bhnc->bhdc', k, v) * scale
        ksum = jnp.sum(k, axis=2) + EPS
        norm = 1.0 / jnp.einsum('bhnd,bhd->bhn', q, ksum)
        out = jnp.einsum('bhnd,bhdc,bhn->bhnc', q, kv, norm)
        return out.transpose(0, 2, 1, 3).reshape(b, n, dim)

    def _L1_ffn_ref(x, router_W, router_b, W1, b1, W2, b2):
        import jax, jax.numpy as jnp
        import numpy as np
        D_MODEL = 128
        D_FF = 512
        N_EXPERTS = 8
        INIT_SCALE = 0.1

        def _trunc_normal(key, shape, std):
            return std * jax.random.truncated_normal(key, -2.0, 2.0, shape, dtype=jnp.float32)
        logits = jnp.einsum('bsd,de->bse', x.astype(jnp.float32), router_W) + router_b
        probs = jax.nn.softmax(logits, axis=-1)
        top1 = jnp.argmax(probs, axis=-1)
        mask = jax.nn.one_hot(top1, N_EXPERTS, dtype=x.dtype)
        gates = mask * probs.astype(x.dtype)
        h = jax.nn.relu(jnp.einsum('bsd,edf->besf', x, W1) + b1[:, None, :])
        y = jnp.einsum('besf,efd->besd', h, W2) + b2[:, None, :]
        out = jnp.einsum('bse,besd->bsd', gates, y)
        return out
    x = L0_attn_x
    xn = _layernorm(x, axis=-1)
    s = _L0_attn_ref(xn, L0_attn_Wq, L0_attn_Wk, L0_attn_Wv)
    g = _silu(_L0_ffn_ref(xn, L0_ffn_gate_w, L0_ffn_gate_b, L0_ffn_w1, L0_ffn_b1, L0_ffn_w2, L0_ffn_b2))
    x = x + s * g
    xn = _layernorm(x, axis=-1)
    s = _L1_attn_ref(xn, L1_attn_W_qkv)
    g = _silu(_L1_ffn_ref(xn, L1_ffn_router_W, L1_ffn_router_b, L1_ffn_W1, L1_ffn_b1, L1_ffn_W2, L1_ffn_b2))
    x = x + s * g
    return x

_drawn_inputs = setup_inputs


def setup_inputs(seed=0):
    import zlib

    import numpy as np

    out = dict(_drawn_inputs(seed))
    spreads = {'L1_ffn_router_b': (0.0, 2.0), 'L1_ffn_b1': (0.0, 2.0), 'L1_ffn_b2': (0.0, 2.0)}
    factors = {'L0_ffn_gate_b': 6.944,
     'L0_ffn_b1': 54.556,
     'L0_ffn_b2': 37.645,
     'L1_attn_W_qkv': 64.0,
     'L1_ffn_router_W': 64.0,
     'L1_ffn_W1': 64.0,
     'L1_ffn_W2': 64.0}
    for name, (base, spread) in spreads.items():
        noise = np.random.default_rng([zlib.crc32(name.encode()), seed]).standard_normal(out[name].shape)
        drawn = base * np.exp(spread * noise) if base else spread * noise
        out[name] = jnp.asarray(drawn.astype(out[name].dtype))
    for name, factor in factors.items():
        out[name] = (out[name] * factor).astype(out[name].dtype)
    return out
```

```python
from contextlib import ExitStack

import concourse.bass as bass
from concourse import mybir

P = 128
ALU = mybir.AluOpType
ACT = mybir.ActivationFunctionType
AX = mybir.AxisListType
F32 = mybir.dt.float32
F16 = mybir.dt.float16
I32 = mybir.dt.int32
U32 = mybir.dt.uint32

RSQRT_SEED = 0x5F3759DF
NEWTON = 3


def past(engine, sem, value):
    if not (isinstance(value, int) and value <= 0):
        engine.wait_ge(sem, value)


def in_pairs(engine, n, body):
    for p in range(2):
        body(p, 0, p)
    with engine.Fori(1, n // 2 - 1) as j:
        for p in range(2):
            body(2 * j + p, j, p)
    for p in range(2):
        body(n - 2 + p, n // 2 - 1, p)


def within(b, n):
    return not isinstance(b, int) or 0 <= b < n


def build(nc, x_d, wq_d, wk_d, wv_d, gate_w, gate_b, ew1, eb1, ew2, eb2, wqkv_d, router_w, router_b,
          fw1, fb1, fw2, fb2, out_d):
    NB, TB, D = x_d.shape
    E, _, FF = ew1.shape
    NH = 16
    DH = D // NH
    K = TB // P
    NT = NB * K
    C = FF // P
    MT = NT + E - 1
    SLOTS = MT * P
    MTP = MT + 1
    LN_EPS, L2_EPS, K_EPS = 1e-5, 1e-12, 1e-6
    QK_SCALE = float(D) ** -0.5
    KV_SCALE = float(DH) ** -0.5
    assert D == P and K == 4 and NB % 2 == 0 and C == 4

    rows_d = [nc.dram_tensor(f"sorted_rows_{l}", (SLOTS, 2 * D), F16, kind="Internal").ap() for l in range(2)]
    y_d = [nc.dram_tensor(f"sorted_y_{l}", (SLOTS, D), F32, kind="Internal").ap() for l in range(2)]

    with ExitStack() as ctx:
        def sb(name, shape, dt):
            return ctx.enter_context(nc.sbuf_tensor(name, shape, dt))

        def sem(name):
            return ctx.enter_context(nc.semaphore(name))

        x_sb = sb("x_sb", [P, NT, D], F32)
        xn16 = sb("xn16", [P, NT, 2, D], F16)
        slots = sb("slots", [P, NB + 2, K * D], F32)
        w1_16 = sb("w1_16", [P, E, 2, FF], F16)
        w2_16 = sb("w2_16", [P, E, 2, C, D], F16)
        bias16 = sb("bias16", [P, E, FF + D], F16)
        w_in = sb("w_in", [P, 2, FF], F32)
        b_in = sb("b_in", [P, FF + D], F32)
        b_hi = sb("b_hi", [P, FF + D], F16)
        second_row = sb("second_row", [P, 1], F32)
        pool_carrier = sb("pool_carrier", [P, 2], F32)
        ident16 = sb("ident16", [P, P], F16)
        ident32 = sb("ident32", [P, P], F32)
        ones16 = sb("ones16", [P, P], F16)
        before16 = sb("before16", [P, P], F16)
        headmask = sb("headmask", [P, P], F32)
        headcol = sb("headcol", [P, NH], F32)
        from_last = sb("from_last", [P, E], F32)
        tile_no = sb("tile_no", [P, MTP], F32)
        ring = sb("ring", [P, 2, K * D], F32)
        wsmall = ring[:, :, :].rearrange("p a n -> p (a n)")[:, 0:6 * D].rearrange("p (i n) -> p i n", i=6)
        m16 = sb("m16", [P, 2, D], F16)
        wv16 = sb("wv16", [P, 2, D], F16)
        wqkv16 = sb("wqkv16", [P, 2, 3 * D], F16)
        rw32 = sb("rw32", [P, 2, E], F32)
        rw16 = sb("rw16", [P, 2, 2, E], F16)
        rbias = sb("rbias", [P, 2, E], F32)
        work = sb("work", [P, 2, K * 2 * D], F32)
        xnf = work[:, 0, :].rearrange("p (b k d) -> p b k d", b=2, k=K)
        tanh = work[:, 1, :].rearrange("p (b k d) -> p b k d", b=2, k=K)
        stats = sb("stats", [P, 2, K, 6], F32)
        mv = sb("mv", [P, 2, K, 2], F32)
        nw_v = sb("nw_v", [P, 2, K], F32)
        nw_y = sb("nw_y", [P, 2, K], F32)
        nw_a = sb("nw_a", [P, 2, K], F32)
        lg = sb("lg", [P, NT, E], F32)
        best = sb("best", [P, NT], F32)
        carrier = sb("carrier", [P, 1], F32)
        expert = sb("expert", [P, NT], F32)
        halfgate = sb("halfgate", [P, NT], F32)
        onehot = sb("onehot", [P, NT, E], F16)
        small = sb("small", [P, 8, E], F32)
        smalli = sb("smalli", [P, 2, E], I32)
        tile_expert = sb("tile_expert", [P, MTP], I32)
        pos = sb("pos", [P, NT], U32)
        pos_io = sb("pos_io", [P, 2, K], U32)
        row_io = sb("row_io", [P, K, D], U32)
        y_back = ring[:, :, :].rearrange("p b (k d) -> p b k d", k=K)
        tv = sb("tv", [P, 4 * 2 * TB // 2], F32)
        t16 = tv[:, 0:2 * TB].bitcast(F16).rearrange("p (b h n) -> p b h n", b=2, h=2)
        v16 = tv[:, 2 * TB:4 * TB].bitcast(F16).rearrange("p (b h k n) -> p b h k n", b=2, h=2, k=K)
        prob = sb("prob", [P, 2, TB], F32)
        pt16 = sb("pt16", [P, 2, 2, K, P], F16)
        tot, incl = prob[:, 0, :], prob[:, 1, :]
        mask = prob[:, 0, :].rearrange("p (t e) -> p t e", e=E)
        cmp = pt16[:, :, :, :, :].rearrange("p a b k n -> p (a b k n)").bitcast(F32)[:, 0:MTP * E].rearrange(
            "p (t e) -> p t e", e=E)
        nmax = sb("nmax", [P, K], F32)
        rsum = sb("rsum", [P, K], F32)
        rden = sb("rden", [P, K], F32)
        qk_n = tv[:, :].rearrange("p (b k n) -> p b k n", b=2, k=K)
        sq = prob[:, :, :].rearrange("p a n -> p (a n)").rearrange("p (k n) -> p k n", k=K)
        sp = work[:, :, :].rearrange("p b (k n) -> p b k n", k=K)
        v_one = sb("v_one", [P, 2, K, D + 2], F32)
        q_t = pt16[:, 0, :, :, :].rearrange("p b k n -> p (b k n)").bitcast(F32)
        kvs = sb("kvs", [P, D + NH], F32)
        ks = sb("ks", [P, 1], F32)
        ss = sb("ss", [P, 3, K * 2 * NH], F32)
        half30 = sb("half30", [P, 1], F32)
        rdn = sb("rdn", [P, K, NH], F32)
        xg = ring[:, 0, :].bitcast(F16).rearrange("p (s h d) -> p s h d", s=4, h=2)
        xgt = sb("xgt", [P, 2, 2, P], F16)
        h32 = pt16[:, :, :, :, :].rearrange("p a b k n -> p (a b k n)").bitcast(F32).rearrange(
            "p (a n) -> p a n", a=2)
        h16 = sb("h16", [P, 4, 2, C, P], F16)
        y_sb = ring[:, 1, :].rearrange("p (s d) -> p s d", s=4)
        zrow = h16[:, :, :, :, :].rearrange("p a b c n -> p (a b c n)").bitcast(F32)[:, 0:SLOTS // P * D // 8]

        bank = ctx.enter_context(nc.psum_tensor("bank", [P, 8, 512], F32))

        s_const = sem("s_const")
        s_zero = sem("s_zero")
        s_zeroed = sem("s_zeroed")
        s_small = sem("s_small")
        s_x = [sem(f"s_x{p}") for p in range(2)]
        s_prep = sem("s_prep")
        s_prep_mm = sem("s_prep_mm")
        s_step = sem("s_step")
        s_out = [sem(f"s_out{p}") for p in range(2)]
        SUMMED = 3
        NORM_STEPS = [2 * K + 3 + 3 * NEWTON, 2 * K + 3 + 3 * NEWTON + SUMMED]
        FIN_STEPS = K + 2
        NAMES = ["w_in", "w_ready", "gathered", "gathered1", "tanh", "norm_step", "xn", "hi", "lo",
                 "xt", "xts", "logits", "lg",  "gate_e", "routed", "rank", "rows_out",
                 "staged", "scat0", "scat1", "scat2", "scat3",
                 "t_mm", "t_hi", "t_lo", "v_mm", "v_hi", "v_lo", "score", "rmax", "expd", "rcp", "pt", "pt_hi",
                 "pt_lo", "pv", "att",
                 "ld0", "ld1", "ld2", "ld3", "xg_t", "xg_s", "up", "h_hi", "h_lo", "down", "y_v",
                 "st0", "st1", "st2", "st3"]
        L = [{n: sem(f"{n}_{l}") for n in NAMES} for l in range(2)]
        LIN = {n: sem(f"lin_{n}") for n in ["qkv", "sq", "v", "step", "rstep", "r0", "qn", "exp", "sp", "kv", "qt", "kvs",
                                            "qts", "out", "att"]}
        FIN = {n: sem(f"fin_{n}") for n in ["g0", "g1", "tanh", "step"]}

        def xnt(l, b):
            i = b + 2 - l
            v = slots[:, i:i + 1, :] if isinstance(i, int) else slots[:, bass.ds(i, 1), :]
            return v.bitcast(F16).rearrange("p o (h n) -> p (o h) n", h=2)

        def att(l, b):
            i = b + 1 - l
            v = slots[:, i:i + 1, :] if isinstance(i, int) else slots[:, bass.ds(i, 1), :]
            return v.rearrange("p o (k d) -> p (o k) d", k=K)

        def tiles(t, b):
            return t[:, bass.ds(K * b, K)] if not isinstance(b, int) else t[:, K * b:K * b + K]

        block = ctx.enter_context(nc.Block())

        @block.sync
        def _(sp_):
            def load_x(b, j, p):
                past(sp_, s_x[p], 16 * j)
                src = x_d[bass.ds(b, 1)] if not isinstance(b, int) else x_d[b:b + 1]
                sp_.dma_start(tiles(x_sb, b), src.rearrange("o (k p) d -> p (o k) d", p=P)).then_inc(s_x[p], 16)

            for b in range(2):
                load_x(b, 0, b)
            for i, w in enumerate((wq_d, wk_d, wv_d)):
                sp_.dma_start(wsmall[:, i, :], w).then_inc(s_small, 16)
            sp_.dma_start(wsmall[:, 3:6, :], wqkv_d.rearrange("(g o) d -> o g d", g=3)).then_inc(s_small, 16)
            for l, (w, b) in enumerate(((gate_w, gate_b), (router_w, router_b))):
                sp_.dma_start(rw32[:, l, :], w).then_inc(s_small, 16)
                sp_.dma_start(rbias[:, l, :], b.rearrange("(o e) -> o e", o=1).to_broadcast([P, E])).then_inc(s_small, 16)
            with sp_.Fori(1, NB // 2) as j:
                for p in range(2):
                    load_x(2 * j + p, j, p)

            def load_weights(l, w1, b1, w2, b2):
                def one(e):
                    def of(t):
                        return t[bass.ds(e, 1)] if not isinstance(e, int) else t[e:e + 1]
                    if l == 1 and isinstance(e, int):
                        sp_.wait_ge(L[0]["w_ready"], 6 * E)
                    past(sp_, L[l]["w_ready"], 6 * e)
                    s = L[l]["w_in"]
                    sp_.dma_start(w_in[:, 0, :], of(w1).rearrange("o d f -> d (o f)")).then_inc(s, 16)
                    sp_.dma_start(w_in[:, 1, :].rearrange("p (c d) -> p c d", c=C),
                                  of(w2).rearrange("o (c p) d -> p (o c) d", p=P)).then_inc(s, 16)
                    for r in (0, 32):
                        sp_.dma_start(b_in[r:r + 1, 0:FF], of(b1)).then_inc(s, 16)
                        sp_.dma_start(b_in[r:r + 1, FF:FF + D], of(b2)).then_inc(s, 16)
                sp_.wait_ge(s_const, 1)
                one(0)
                with sp_.Fori(1, E) as e:
                    one(e)

            load_weights(0, ew1, eb1, ew2, eb2)
            sp_.wait_ge(s_zero, 1)
            for l in range(2):
                sp_.dma_start(rows_d[l].bitcast(F32).rearrange("(p a r) d -> p a (r d)", p=P, a=1).rearrange(
                    "p a (c n) -> p (a c) n", c=8),
                    zrow.unsqueeze(1).to_broadcast([P, 8, zrow.shape[1]])).then_inc(s_zeroed, 16)

            def experts(l):
                def step(s, j, r):
                    if within(s, MT):
                        past(sp_, L[l]["xg_t"], s - 3)
                        src = rows_d[l][bass.ds(s * P, P)] if not isinstance(s, int) else rows_d[l][s * P:s * P + P]
                        sp_.dma_start(xg[:, r, :, :], src.rearrange("p (h d) -> p h d", h=2)).then_inc(
                            L[l][f"ld{r}"], 16)
                    if within(s - 7, MT):
                        u, ru = s - 7, (r + 1) % 4
                        sp_.wait_ge(L[l]["y_v"], u + 1)
                        dst = y_d[l][bass.ds(u * P, P)] if not isinstance(u, int) else y_d[l][u * P:u * P + P]
                        sp_.dma_start(dst, y_sb[:, ru, :]).then_inc(L[l][f"st{ru}"], 16)
                for k in range(4):
                    sp_.wait_ge(L[l][f"scat{k}"], 16 * NB)
                for s in range(8):
                    step(s, s // 4, s % 4)
                with sp_.Fori(2, MT // 4) as j:
                    for r in range(4):
                        step(4 * j + r, j, r)
                for s in range(MT // 4 * 4, MT + 7):
                    step(s, s // 4, s % 4)

            experts(0)
            load_weights(1, fw1, fb1, fw2, fb2)
            experts(1)

            def store(b, j, p):
                sp_.wait_ge(FIN["step"], FIN_STEPS * (b + 1))
                dst = out_d[bass.ds(b, 1)] if not isinstance(b, int) else out_d[b:b + 1]
                sp_.dma_start(dst.rearrange("o (k p) d -> p (o k) d", p=P), tiles(x_sb, b)).then_inc(s_out[p], 16)
            in_pairs(sp_, NB, store)
            for p in range(2):
                sp_.wait_ge(s_out[p], 16 * NB // 2)

        @block.gpsimd
        def _(pool):
            g = nc.gpsimd
            g.memset(pool_carrier[:], 0.0)
            g.memset(b_in[:], 0.0).then_inc(s_const, 1)
            g.memset(zrow, 0.0).then_inc(s_zero, 1)
            g.memset(ones16[:], 1.0).then_inc(s_const, 1)
            g.memset(second_row[:], 1.0).then_inc(s_const, 1)
            g.memset(ident32[:], 0.0).then_inc(s_const, 1)
            g.memset(headmask[:], KV_SCALE).then_inc(s_const, 1)
            g.memset(headcol[:], 1.0).then_inc(s_const, 1)
            g.memset(v_one[:], 1.0).then_inc(s_const, 1)
            g.iota(from_last[:], [[-1, E]], base=E, channel_multiplier=0,
                   allow_small_or_imprecise_dtypes=True).then_inc(s_const, 1)
            g.iota(tile_no[:], [[1, MTP]], base=0, channel_multiplier=0,
                   allow_small_or_imprecise_dtypes=True).then_inc(s_const, 1)
            pool.wait_ge(s_const, 9)
            g.affine_select(out=ident32[:], in_=ident32[:], compare_op=ALU.not_equal, fill=1.0, base=0,
                            pattern=[[-1, P]], channel_multiplier=1).then_inc(s_const, 1)
            g.affine_select(out=before16[:], in_=ones16[:], compare_op=ALU.is_gt, fill=0.0, base=0,
                            pattern=[[1, P]], channel_multiplier=-1).then_inc(s_const, 1)
            hm = headmask[:, :].rearrange("p (h d) -> p h d", h=NH)
            g.affine_select(out=hm, in_=hm, compare_op=ALU.is_ge, fill=0.0, base=0,
                            pattern=[[-DH, NH], [0, DH]], channel_multiplier=1).then_inc(s_const, 1)
            g.affine_select(out=headcol[:], in_=headcol[:], compare_op=ALU.is_ge, fill=0.0, base=0,
                            pattern=[[-DH, NH]], channel_multiplier=1).then_inc(s_const, 1)
            g.affine_select(out=second_row[:], in_=second_row[:], compare_op=ALU.is_ge, fill=0.0, base=-32,
                            pattern=[[0, 1]], channel_multiplier=1).then_inc(s_const, 1)
            pool.wait_ge(s_const, 14)
            g.affine_select(out=hm, in_=hm, compare_op=ALU.is_ge, fill=0.0, base=DH - 1,
                            pattern=[[DH, NH], [0, DH]], channel_multiplier=-1).then_inc(s_const, 1)
            g.affine_select(out=headcol[:], in_=headcol[:], compare_op=ALU.is_ge, fill=0.0, base=DH - 1,
                            pattern=[[DH, NH]], channel_multiplier=-1).then_inc(s_const, 1)
            g.tensor_copy(ident16[:], ident32[:]).then_inc(s_const, 1)

            def carry():
                g.tensor_tensor(pool_carrier[:, 1:2], pool_carrier[:, 0:1], pool_carrier[:, 0:1], ALU.add)

            def expert_weights(l, e):
                def of(t):
                    return t[:, bass.ds(e, 1)] if not isinstance(e, int) else t[:, e:e + 1]
                pool.wait_ge(L[l]["w_in"], 96 * (e + 1))
                w1o = of(w1_16)
                w2o = of(w2_16).rearrange("p o h c d -> p o h (c d)")
                bo = of(bias16)
                w1i, w2i = w_in[:, 0:1, :], w_in[:, 1:2, :]
                bi = b_in[:, :].unsqueeze(1)
                r = L[l]["w_ready"]
                g.tensor_copy(w1o[:, :, 0, :], w1i).then_inc(r, 1)
                g.tensor_copy(w2o[:, :, 0, :], w2i).then_inc(r, 1)
                g.tensor_scalar(b_hi[:], b_in[:], second_row[:, 0:1], None, ALU.mult).then_inc(r, 1)
                pool.wait_ge(r, 6 * e + 3)
                g.tensor_tensor(w1o[:, :, 1, :], w1i, w1o[:, :, 0, :], ALU.subtract).then_inc(r, 1)
                g.tensor_tensor(w2o[:, :, 1, :], w2i, w2o[:, :, 0, :], ALU.subtract).then_inc(r, 1)
                g.tensor_tensor(bo, bi, b_hi[:, :].unsqueeze(1), ALU.subtract).then_inc(r, 1)
                pool.wait_ge(r, 6 * e + 6)

            def fetch(b, j, p, ysrc, done, freed, per, at):
                past(pool, freed, per * (b - 2) + at)
                src = tiles(pos, b)
                g.tensor_copy(pos_io[:, p, :], src).then_inc(s_posio[0], 1)
                pool.wait_ge(s_posio[0], s_posio[1] + b + 1)
                carry()
                for k in range(K):
                    g.indirect_dma_start(y_back[:, p, k, :], None, ysrc[:, :],
                                         bass.IndirectOffsetOnAxis(pos_io[:, p, k:k + 1], 0)).then_inc(done[p], 16)

            def norm_stage(l):
                def body(b, j, p):
                    if l == 1:
                        if isinstance(b, int) and b == 0:
                            for bb in range(2):
                                fetch(bb, 0, bb, y_d[0], [L[1]["gathered"], L[1]["gathered1"]], L[1]["norm_step"],
                                  NORM_STEPS[1], SUMMED)
                        if within(b + 2, NB):
                            fetch(b + 2, j + 1, p, y_d[0], [L[1]["gathered"], L[1]["gathered1"]], L[1]["norm_step"],
                                  NORM_STEPS[1], SUMMED)
                    pool.wait_ge(L[l]["hi"], b + 1)
                    hl = tiles(xn16, b)
                    g.tensor_tensor(hl[:, :, 1, :], xnf[:, p, :, :], hl[:, :, 0, :], ALU.subtract).then_inc(
                        L[l]["lo"], 1)
                    if p == 0:
                        expert_weights(l, j)
                in_pairs(pool, NB, body)

            def scatter(l):
                pool.wait_ge(L[l]["routed"], 2)
                if l == 0:
                    pool.wait_ge(s_zeroed, 32)

                def body(b, first):
                    for k in range(K):
                        if not first:
                            pool.wait_ge(L[l][f"scat{k}"], 16 * b)
                    st = L[l]["staged"]
                    g.tensor_copy(pos_io[:, 0, :], tiles(pos, b)).then_inc(st, 1)
                    g.tensor_copy(row_io[:, :, :], tiles(xn16, b).rearrange("p k h d -> p k (h d)").bitcast(U32)
                                  ).then_inc(st, 1)
                    pool.wait_ge(st, 2 * b + 2)
                    carry()
                    for k in range(K):
                        g.indirect_dma_start(rows_d[l][:, :], bass.IndirectOffsetOnAxis(pos_io[:, 0, k:k + 1], 0),
                                             row_io[:, k, :].bitcast(F16), None).then_inc(L[l][f"scat{k}"], 16)
                body(0, True)
                with pool.Fori(1, NB) as b:
                    body(b, False)

            s_posio = [sem("s_posio_a"), 0]
            norm_stage(0)
            scatter(0)
            for r in range(4):
                pool.wait_ge(L[0][f"st{r}"], 16 * len(range(r, MT, 4)))
            norm_stage(1)
            scatter(1)
            for r in range(4):
                pool.wait_ge(L[1][f"st{r}"], 16 * len(range(r, MT, 4)))
            s_posio = [sem("s_posio_b"), 0]
            for bb in range(2):
                fetch(bb, 0, bb, y_d[1], [FIN["g0"], FIN["g1"]], FIN["step"], FIN_STEPS, 1)
            with pool.Fori(1, NB // 2) as j:
                for p in range(2):
                    fetch(2 * j + p, j, p, y_d[1], [FIN["g0"], FIN["g1"]], FIN["step"], FIN_STEPS, 1)

        @block.scalar
        def _(act):
            a = nc.scalar

            def norm_stage(l):
                S = L[l]

                def t_hyp(b, j, p):
                    act.wait_ge(S["gathered1" if p else "gathered"], 64 * (j + 1))
                    past(act, S["norm_step"], NORM_STEPS[1] * (b - 2) + SUMMED)
                    a.activation(tanh[:, p, :, :], y_back[:, p, :, :], ACT.Tanh).then_inc(S["tanh"], 1)

                def body(b, j, p):
                    if l == 1:
                        if isinstance(b, int) and b == 0:
                            t_hyp(0, 0, 0)
                        if within(b + 1, NB):
                            t_hyp(b + 1, j + p, 1 - p)
                    act.wait_ge(S["xn"], K * (b + 1))
                    hl = tiles(xn16, b)
                    a.activation(hl[:, :, 0, :], xnf[:, p, :, :], ACT.Copy).then_inc(S["hi"], 1)
                    if within(b - 1, NB):
                        to_sbuf(b - 1, 1 - p)

                def to_sbuf(b, p):
                    act.wait_ge(S["xt"], b + 1)
                    a.activation(xnt(l, b), bank[:, p, :].bitcast(F16).rearrange("p (h n) -> p h n", h=2),
                                 ACT.Copy).then_inc(S["xts"], 1)

                in_pairs(act, NB, body)
                to_sbuf(NB - 1, 1)
                if l == 1:
                    act.wait_ge(S["lg"], NB + 1)
                    a.activation(lg[:], lg[:], ACT.Exp).then_inc(S["gate_e"], 1)

            def attention():
                S = L[0]

                def t_high(b, p):
                    act.wait_ge(S["t_mm"], b + 1)
                    a.activation(t16[:, p, 0, :], bank[:, 7, :], ACT.Copy).then_inc(S["t_hi"], 1)

                def v_high(b, p):
                    act.wait_ge(S["v_mm"], b + 1)
                    a.activation(v16[:, p, 0, :, :], bank[:, 7, :].rearrange("p (k d) -> p k d", k=K),
                                 ACT.Copy).then_inc(S["v_hi"], 1)

                def softmax_exp(u, q):
                    act.wait_ge(S["rmax"], u + 1)
                    past(act, S["pt"], u - 1)
                    a.activation(prob[:, q % 2, :], bank[:, q, :], ACT.Exp, bias=nmax[:, q:q + 1],
                                 accum_out=rsum[:, q:q + 1]).then_inc(S["expd"], 1)

                def result(b, u, q):
                    act.wait_ge(S["rcp"], u + 1)
                    act.wait_ge(S["pv"], u + 1)
                    a.activation(att(0, b)[:, q, :], bank[:, 6, 0:D], ACT.Copy,
                                 scale=rden[:, q:q + 1]).then_inc(S["att"], 1)

                t_high(0, 0)
                v_high(0, 0)
                softmax_exp(0, 0)

                def body(b, j, p):
                    for q in range(K):
                        u = K * b + q
                        if q == 0 and within(b + 1, NB):
                            t_high(b + 1, 1 - p)
                        if q == 2 and within(b + 1, NB):
                            v_high(b + 1, 1 - p)
                        if within(u - 2, NT):
                            result(b if q >= 2 else b - 1, u - 2, (q + 2) % K)
                        if within(u + 1, NT):
                            softmax_exp(u + 1, (q + 1) % K)
                        act.wait_ge(S["pt"], u + 1)
                        past(act, S["pv"], u - 1)
                        a.activation(pt16[:, q % 2, 0, :, :],
                                     bank[:, 4 + q % 2, :].rearrange("p (k n) -> p k n", k=K),
                                     ACT.Copy).then_inc(S["pt_hi"], 1)
                in_pairs(act, NB, body)
                result(NB - 1, NT - 2, 2)
                result(NB - 1, NT - 1, 3)

            def linear_attention():
                S = LIN

                def front(b, p):
                    act.wait_ge(S["qkv"], b + 1)
                    qkv = bank[:, 0:K, :]
                    past(act, S["step"], 5 * (b - 1) + 1)
                    a.activation(sq, qkv[:, :, 0:2 * D], ACT.Square).then_inc(S["sq"], 1)
                    past(act, S["kv"], b - 1)
                    a.activation(v_one[:, p, :, 0:D], qkv[:, :, 2 * D:3 * D], ACT.Copy).then_inc(S["v"], 1)

                def inv_norm(b):
                    act.wait_ge(S["step"], 5 * b + 2)
                    a.activation(ss[:, 1, :], ss[:, 0, :], ACT.Ln, scale=2.0 ** 30).then_inc(S["r0"], 1)
                    act.wait_ge(S["r0"], 2 * b + 1)
                    a.activation(ss[:, 1, :], ss[:, 1, :], ACT.Exp, scale=-0.5, bias=half30[:, 0:1]).then_inc(S["r0"], 1)

                def softplus(b, p):
                    act.wait_ge(S["qn"], b + 1)
                    a.activation(qk_n[:, p, :, :], qk_n[:, p, :, :], ACT.Exp).then_inc(S["exp"], 1)
                    act.wait_ge(S["exp"], b + 1)
                    past(act, S["kv"], b - 1)
                    past(act, S["qt"], b - 1)
                    a.activation(sp[:, p, :, :], qk_n[:, p, :, :], ACT.Ln, bias=1.0).then_inc(S["sp"], 1)

                def q_out(b):
                    act.wait_ge(S["qt"], b + 1)
                    past(act, S["out"], b)
                    a.activation(q_t[:, :], bank[:, 5, :], ACT.Copy).then_inc(S["qts"], 1)

                def body(b, j, p):
                    front(b, p)
                    if within(b - 1, NB):
                        softplus(b - 1, 1 - p)
                    inv_norm(b)
                    if within(b - 1, NB):
                        q_out(b - 1)
                in_pairs(act, NB, body)
                softplus(NB - 1, 1)
                q_out(NB - 1)

            def experts(l):
                S = L[l]

                def step(s, r):
                    u, ru = s - 1, (r + 3) % 4
                    if within(u, MT):
                        act.wait_ge(S["up"], u + 1)
                        past(act, S["h_lo"], u - 1)
                        past(act, S["down"], u - 3)
                        h = bank[:, 2 + ru % 2, :].rearrange("p (c n) -> p c n", c=C)
                        f = ACT.Gelu if l == 0 else ACT.Relu
                        a.activation(h16[:, ru, 0, :, :], h, f).then_inc(S["h_hi"], 1)
                        if l == 0:
                            a.activation(h32[:, ru % 2, :].rearrange("p (c n) -> p c n", c=C), h,
                                         f).then_inc(S["h_hi"], 1)
                if l == 0:
                    act.wait_ge(s_zeroed, 32)
                for s in range(8):
                    step(s, s % 4)
                with act.Fori(2, MT // 4) as j:
                    for r in range(4):
                        step(4 * j + r, r)
                for s in range(MT // 4 * 4, MT + 1):
                    step(s, s % 4)

            def final():
                def body(b, j, p):
                    act.wait_ge(FIN["g1" if p else "g0"], 64 * (j + 1))
                    past(act, FIN["step"], FIN_STEPS * (b - 2) + FIN_STEPS)
                    hg = tiles(halfgate, b)
                    for k in range(K):
                        a.activation(tanh[:, p, k, :], y_back[:, p, k, :], ACT.Tanh,
                                     scale=hg[:, k:k + 1]).then_inc(FIN["tanh"], 1)
                in_pairs(act, NB, body)

            norm_stage(0)
            attention()
            experts(0)
            norm_stage(1)
            linear_attention()
            experts(1)
            final()

        @block.vector
        def _(dve):
            v = nc.vector
            count = [0]

            def link(ins):
                count[0] += 1
                ins.then_inc(s_step, 1)
                dve.wait_ge(s_step, count[0])

            def pair(dst, src):
                link(v.tensor_copy(dst[:, 0], src))
                v.tensor_tensor(dst[:, 1], src, dst[:, 0], ALU.subtract).then_inc(s_prep, 1)

            v.memset(half30[:], 15.0 * 0.6931471805599453).then_inc(s_prep, 1)
            dve.wait_ge(s_small, 16 * 8)
            for l in range(2):
                pair(rw16[:, l], rw32[:, l, :])
            dve.wait_ge(s_prep_mm, 1)
            link(v.tensor_scalar(wsmall[:, 0, :], bank[:, 4, 0:D], QK_SCALE, None, ALU.mult))
            pair(m16, wsmall[:, 0, :])
            dve.wait_ge(s_prep_mm, 2)
            pair(wv16, bank[:, 5, 0:D])
            dve.wait_ge(s_prep_mm, 3)
            pair(wqkv16, bank[:, 6, 0:3 * D])

            def norm_stage(l):
                S = L[l]
                STEPS = NORM_STEPS[l]

                def body(b, j, p):
                    n = [0]

                    def step(ins, wait=True):
                        n[0] += 1
                        ins.then_inc(S["norm_step"], 1)
                        if wait:
                            dve.wait_ge(S["norm_step"], STEPS * b + n[0])

                    x = tiles(x_sb, b)
                    if l == 0:
                        dve.wait_ge(s_x[p], 16 * (j + 1))
                    else:
                        dve.wait_ge(S["tanh"], b + 1)
                        t = tanh[:, p, :, :]
                        step(v.scalar_tensor_tensor(out=t, in0=t, scalar=1.0, in1=y_back[:, p, :, :],
                                                    op0=ALU.add, op1=ALU.mult))
                        step(v.tensor_tensor(t, t, att(0, b), ALU.mult))
                        step(v.tensor_tensor(x, x, t, ALU.add))
                    v.memset(carrier[:], 0.0)
                    for k in range(K):
                        step(v.bn_stats(stats[:, p, k, :], x[:, k, :]), wait=k == K - 1)
                    v.memset(carrier[:], 0.0)
                    for k in range(K):
                        step(v.bn_aggr(mv[:, p, k, :], stats[:, p, k, :]), wait=k == K - 1)
                    vv, y, w = nw_v[:, p, :], nw_y[:, p, :], nw_a[:, p, :]
                    step(v.tensor_scalar(vv, mv[:, p, :, 1], LN_EPS, None, ALU.add))
                    step(v.tensor_scalar(w.bitcast(I32), vv.bitcast(I32), 1, None, ALU.arith_shift_right))
                    step(v.tensor_scalar(y.bitcast(I32), w.bitcast(I32), -1.0, float(RSQRT_SEED), ALU.mult, ALU.add))
                    for _ in range(NEWTON):
                        step(v.tensor_tensor(w, y, y, ALU.mult))
                        step(v.scalar_tensor_tensor(out=w, in0=w, scalar=-0.5, in1=vv, op0=ALU.mult, op1=ALU.mult))
                        step(v.scalar_tensor_tensor(out=y, in0=w, scalar=1.5, in1=y, op0=ALU.add, op1=ALU.mult))
                    assert n[0] == STEPS
                    past(dve, S["lo"], b - 1)
                    for k in range(K):
                        v.tensor_scalar(xnf[:, p, k, :], x[:, k, :], mv[:, p, k, 0:1], nw_y[:, p, k:k + 1],
                                        ALU.subtract, ALU.mult).then_inc(S["xn"], 1)
                    if within(b - 1, NB):
                        keep_logits(b - 1, 1 - p)

                def keep_logits(b, p):
                    dve.wait_ge(S["logits"], b + 1)
                    v.tensor_tensor(tiles(lg, b), bank[:, 2 + p, 0:K * E].rearrange("p (k e) -> p k e", k=K),
                                    rbias[:, l, :].unsqueeze(1).to_broadcast([P, K, E]), ALU.add).then_inc(S["lg"], 1)

                in_pairs(dve, NB, body)
                keep_logits(NB - 1, 1)

            def routing(l):
                S = L[l]
                dve.wait_ge(S["lg"], NB)
                wide = [P, NT, E]

                def spread(t):
                    return t.unsqueeze(2).to_broadcast(wide)

                def top(values):
                    link(v.tensor_reduce(best[:], values, AX.X, ALU.max))
                    link(v.tensor_tensor(mask, values, spread(best[:]), ALU.is_equal))
                    link(v.tensor_tensor(mask, mask, from_last[:].unsqueeze(1).to_broadcast(wide), ALU.mult))

                top(lg[:])
                link(v.tensor_reduce(expert[:], mask, AX.X, ALU.max))
                if l == 0:
                    link(v.tensor_tensor(mask, from_last[:].unsqueeze(1).to_broadcast(wide), spread(expert[:]),
                                         ALU.is_equal))
                    link(v.scalar_tensor_tensor(out=lg[:], in0=mask, scalar=-3.0e38, in1=lg[:], op0=ALU.mult,
                                                op1=ALU.add))
                    top(lg[:])
                    link(v.tensor_reduce(best[:], mask, AX.X, ALU.max))
                    link(v.tensor_tensor(expert[:], expert[:], best[:], ALU.min))
                else:
                    v.tensor_tensor(lg[:], lg[:], spread(best[:]), ALU.subtract).then_inc(S["lg"], 1)
                v.tensor_tensor(onehot[:], expert[:].unsqueeze(2).to_broadcast([P, NT, E]),
                                from_last[:].unsqueeze(1).to_broadcast([P, NT, E]), ALU.is_equal).then_inc(S["routed"], 1)
                dve.wait_ge(S["rank"], 1)
                by_expert = tot.rearrange("p (e t) -> p t e", e=E)
                link(v.tensor_copy(by_expert, bank[:, 5, :].rearrange("p (t e) -> p t e", e=E)))
                link(v.tensor_tensor_scan(incl, tot, tot, 0.0, ALU.add, ALU.max))
                inc_v = incl.rearrange("p (e t) -> p e t", e=E)
                ends = inc_v[:, :, NT - 1]
                start, n, nt, tc, delta = (small[:, i, :] for i in range(5))
                link(v.memset(start, 0.0))
                link(v.tensor_copy(start[:, 1:E], ends[:, 0:E - 1]))
                link(v.tensor_tensor(n, ends, start, ALU.subtract))
                link(v.tensor_scalar(smalli[:, 0, :], n, float(P - 1), None, ALU.add))
                link(v.tensor_scalar(smalli[:, 1, :], smalli[:, 0, :], 7, None, ALU.arith_shift_right))
                link(v.tensor_copy(nt, smalli[:, 1, :]))
                link(v.tensor_tensor_scan(tc, nt, nt, 0.0, ALU.add, ALU.max))
                link(v.tensor_tensor(delta, tc, nt, ALU.subtract))
                link(v.scalar_tensor_tensor(out=delta, in0=delta, scalar=float(P), in1=start, op0=ALU.mult,
                                            op1=ALU.subtract))
                link(v.tensor_tensor(incl, incl, tot, ALU.subtract))
                link(v.tensor_tensor(inc_v, inc_v, delta.unsqueeze(2).to_broadcast([P, E, NT]), ALU.add))
                te = incl.rearrange("p (e t) -> p t e", e=E)
                tt = tot.rearrange("p (t e) -> p t e", e=E)
                link(v.tensor_tensor(tt, te, bank[:, 4, :].rearrange("p (t e) -> p t e", e=E), ALU.add))
                link(v.tensor_tensor(tt, tt, onehot[:], ALU.mult))
                with nc.allow_low_precision(reason="whole numbers below 2^24, summed in float32"):
                    v.tensor_reduce(pos[:], tt, AX.X, ALU.add).then_inc(S["routed"], 1)
                link(v.tensor_tensor(cmp, tile_no[:].unsqueeze(2).to_broadcast([P, MTP, E]),
                                     tc.unsqueeze(1).to_broadcast([P, MTP, E]), ALU.is_ge))
                link(v.tensor_reduce(incl[:, 0:MTP], cmp, AX.X, ALU.add))
                v.tensor_scalar(tile_expert[:], incl[:, 0:MTP], float(E - 1), None, ALU.min).then_inc(S["routed"], 1)
                if l == 1:
                    dve.wait_ge(S["gate_e"], 1)
                    link(v.tensor_reduce(halfgate[:], lg[:], AX.X, ALU.add))
                    link(v.reciprocal(halfgate[:], halfgate[:]))
                    link(v.tensor_scalar(halfgate[:], halfgate[:], 0.5, None, ALU.mult))

            def attention():
                S = L[0]

                def t_low(b, p):
                    dve.wait_ge(S["t_hi"], b + 1)
                    v.tensor_tensor(t16[:, p, 1, :], bank[:, 7, :], t16[:, p, 0, :], ALU.subtract).then_inc(S["t_lo"], 1)

                def v_low(b, p):
                    dve.wait_ge(S["v_hi"], b + 1)
                    v.tensor_tensor(v16[:, p, 1, :, :], bank[:, 7, :].rearrange("p (k d) -> p k d", k=K),
                                    v16[:, p, 0, :, :], ALU.subtract).then_inc(S["v_lo"], 1)

                def row_max(u, q):
                    dve.wait_ge(S["score"], u + 1)
                    past(dve, S["expd"], u - 3)
                    v.tensor_reduce(nmax[:, q:q + 1], bank[:, q, :], AX.X, ALU.max, negate=True).then_inc(S["rmax"], 1)

                t_low(0, 0)
                v_low(0, 0)
                row_max(0, 0)
                row_max(1, 1)

                def body(b, j, p):
                    for q in range(K):
                        u = K * b + q
                        if within(u + 2, NT):
                            row_max(u + 2, (q + 2) % K)
                        if q == 0 and within(b + 1, NB):
                            t_low(b + 1, 1 - p)
                        if q == 2 and within(b + 1, NB):
                            v_low(b + 1, 1 - p)
                        dve.wait_ge(S["expd"], u + 1)
                        past(dve, S["att"], u - 3)
                        v.reciprocal(rden[:, q:q + 1], rsum[:, q:q + 1]).then_inc(S["rcp"], 1)
                        dve.wait_ge(S["pt_hi"], u + 1)
                        v.tensor_tensor(pt16[:, q % 2, 1, :, :],
                                        bank[:, 4 + q % 2, :].rearrange("p (k n) -> p k n", k=K),
                                        pt16[:, q % 2, 0, :, :], ALU.subtract).then_inc(S["pt_lo"], 1)
                in_pairs(dve, NB, body)

            def linear_attention():
                S = LIN
                def at(b, n):
                    return 5 * b + n

                def front(b, p):
                    dve.wait_ge(S["sq"], b + 1)
                    st = S["step"]
                    norm2, r, w = ss[:, 0, :], ss[:, 1, :], ss[:, 2, :]
                    v.tensor_reduce(norm2.rearrange("p (k h) -> p k h", k=K),
                                    sq.rearrange("p k (h d) -> p k h d", d=DH), AX.X, ALU.add).then_inc(st, 1)
                    dve.wait_ge(st, at(b, 1))
                    v.tensor_scalar(norm2, norm2, L2_EPS * L2_EPS, None, ALU.max).then_inc(st, 1)

                def normalise(b, p):
                    st = S["step"]
                    norm2, r, w = ss[:, 0, :], ss[:, 1, :], ss[:, 2, :]
                    dve.wait_ge(S["r0"], 2 * b + 2)
                    v.tensor_tensor(w, r, r, ALU.mult).then_inc(st, 1)
                    dve.wait_ge(st, at(b, 3))
                    v.scalar_tensor_tensor(out=w, in0=w, scalar=-0.5, in1=norm2, op0=ALU.mult,
                                           op1=ALU.mult).then_inc(st, 1)
                    dve.wait_ge(st, at(b, 4))
                    v.scalar_tensor_tensor(out=r, in0=w, scalar=1.5, in1=r, op0=ALU.add, op1=ALU.mult).then_inc(st, 1)
                    dve.wait_ge(st, at(b, 5))
                    dve.wait_ge(S["v"], b + 1)
                    rr = r.rearrange("p (k h) -> p k h", k=K)
                    for k in range(K):
                        ins = v.tensor_tensor(qk_n[:, p, k, :].rearrange("p (h d) -> p h d", d=DH),
                                              bank[:, k, 0:2 * D].rearrange("p (h d) -> p h d", d=DH),
                                              rr[:, k, :].unsqueeze(2).to_broadcast([P, 2 * NH, DH]), ALU.mult)
                    ins.then_inc(S["qn"], 1)

                def state(b):
                    dve.wait_ge(S["kv"], b + 1)
                    past(dve, S["out"], b)
                    st = S["rstep"]
                    v.tensor_scalar(ks[:], bank[:, 4, D:D + 1], K_EPS * 1.0, None, ALU.add).then_inc(st, 1)
                    v.tensor_tensor(kvs[:, 0:D], bank[:, 4, 0:D], headmask[:], ALU.mult).then_inc(st, 1)
                    dve.wait_ge(st, 4 * b + 2)
                    v.tensor_scalar(kvs[:, D:D + NH], headcol[:], ks[:, 0:1], None, ALU.mult).then_inc(S["kvs"], 1)

                def result(b, j, p):
                    dve.wait_ge(S["out"], b + 1)
                    st = S["rstep"]
                    o = bank[:, 6:8, 0:2 * (D + NH)].rearrange("p a (k n) -> p a k n", k=2)
                    for i in range(2):
                        v.reciprocal(rdn[:, 2 * i:2 * i + 2, :], o[:, i, :, D:D + NH]).then_inc(st, 1)
                    dve.wait_ge(st, 4 * b + 4)
                    dst = att(1, b)
                    for k in range(K):
                        ins = v.tensor_tensor(dst[:, k, :].rearrange("p (h d) -> p h d", d=DH),
                                              o[:, k // 2, k % 2, 0:D].rearrange("p (h d) -> p h d", d=DH),
                                              rdn[:, k, :].unsqueeze(2).to_broadcast([P, NH, DH]), ALU.mult)
                    ins.then_inc(S["att"], 1)

                def body(b, j, p):
                    front(b, p)
                    if within(b - 1, NB):
                        state(b - 1)
                    normalise(b, p)
                    if within(b - 1, NB):
                        result(b - 1, j, 1 - p)
                in_pairs(dve, NB, body)
                state(NB - 1)
                result(NB - 1, 0, 1)

            def experts(l):
                S = L[l]

                def step(s, j, r):
                    if within(s, MT):
                        dve.wait_ge(S["xg_t"], s + 1)
                        past(dve, S["up"], s - 1)
                        v.tensor_copy(xgt[:, r % 2, :, :],
                                      bank[:, r % 2, 0:P].bitcast(F16).rearrange("p (h n) -> p h n", h=2)
                                      ).then_inc(S["xg_s"], 1)
                    if within(s - 1, MT):
                        u, ru = s - 1, (r + 3) % 4
                        h = bank[:, 2 + ru % 2, :].rearrange("p (c n) -> p c n", c=C)
                        if l == 0:
                            dve.wait_ge(S["h_hi"], 2 * u + 2)
                            v.tensor_tensor(h16[:, ru, 1, :, :], h32[:, ru % 2, :].rearrange("p (c n) -> p c n", c=C),
                                            h16[:, ru, 0, :, :], ALU.subtract).then_inc(S["h_lo"], 1)
                        else:
                            dve.wait_ge(S["h_hi"], u + 1)
                            v.scalar_tensor_tensor(out=h16[:, ru, 1, :, :], in0=h, scalar=0.0, in1=h16[:, ru, 0, :, :],
                                                   op0=ALU.max, op1=ALU.subtract).then_inc(S["h_lo"], 1)
                    if within(s - 3, MT):
                        u, ru = s - 3, (r + 1) % 4
                        dve.wait_ge(S["down"], u + 1)
                        ju = j - 1 if r != 3 else j
                        past(dve, S[f"st{ru}"], 16 * ju)
                        v.tensor_copy(y_sb[:, ru, :], bank[:, 4 + ru % 2, 0:D]).then_inc(S["y_v"], 1)
                for s in range(8):
                    step(s, s // 4, s % 4)
                with dve.Fori(2, MT // 4) as j:
                    for r in range(4):
                        step(4 * j + r, j, r)
                for s in range(MT // 4 * 4, MT + 3):
                    step(s, s // 4, s % 4)

            def final():
                def body(b, j, p):
                    dve.wait_ge(FIN["tanh"], K * (b + 1))
                    t = tanh[:, p, :, :]
                    st = FIN["step"]
                    N = FIN_STEPS
                    v.scalar_tensor_tensor(out=t, in0=t, scalar=1.0, in1=y_back[:, p, :, :],
                                           op0=ALU.add, op1=ALU.mult).then_inc(st, 1)
                    dve.wait_ge(st, N * b + 1)
                    hg, s1, x = tiles(halfgate, b), att(1, b), tiles(x_sb, b)
                    for k in range(K):
                        v.scalar_tensor_tensor(out=t[:, k, :], in0=t[:, k, :], scalar=hg[:, k:k + 1], in1=s1[:, k, :],
                                               op0=ALU.mult, op1=ALU.mult).then_inc(st, 1)
                    dve.wait_ge(st, N * b + 1 + K)
                    v.tensor_tensor(x, x, t, ALU.add).then_inc(st, 1)
                in_pairs(dve, NB, body)

            norm_stage(0)
            routing(0)
            attention()
            experts(0)
            norm_stage(1)
            routing(1)
            linear_attention()
            experts(1)
            final()

        @block.tensor
        def _(pe):
            def product(out, left, right, start=True, stop=True):
                pe.matmul(out, left(0), right(0), start=start, stop=False)
                pe.matmul(out, left(0), right(1), start=False, stop=False)
                return pe.matmul(out, left(1), right(0), start=False, stop=stop)

            pe.wait_ge(s_small, 16 * 8)
            pe.matmul(bank[:, 4, 0:D], wsmall[:, 0, :], wsmall[:, 1, :], start=True, stop=True).then_inc(s_prep_mm, 1)
            pe.wait_ge(s_const, 17)
            pe.transpose(bank[:, 5, 0:D], wsmall[:, 2, :], ident32[:]).then_inc(s_prep_mm, 1)
            for i in range(3):
                m = pe.transpose(bank[:, 6, i * D:i * D + D], wsmall[:, 3 + i, :], ident32[:])
            m.then_inc(s_prep_mm, 1)

            def norm_stage(l):
                S = L[l]

                def turn(b, p):
                    pe.wait_ge(S["lo"], b + 1)
                    past(pe, S["xts"], b - 1)
                    dst = bank[:, p, :].bitcast(F16).rearrange("p (h k n) -> p h k n", h=2, k=K)
                    hl = tiles(xn16, b)
                    for h in range(2):
                        for k in range(K):
                            m = pe.transpose(dst[:, h, k, :], hl[:, k, h, :], ident16[:])
                    m.then_inc(S["xt"], 1)

                def logits(b, p):
                    pe.wait_ge(S["xts"], b + 1)
                    past(pe, S["lg"], b - 1)
                    x = xnt(l, b)
                    for k in range(K):
                        m = product(bank[:, 2 + p, k * E:k * E + E], lambda h: x[:, h, k * P:k * P + P],
                                    lambda h: rw16[:, l, h, :])
                    m.then_inc(S["logits"], 1)

                def body(b, j, p):
                    turn(b, p)
                    if within(b - 1, NB):
                        logits(b - 1, 1 - p)
                if l == 0:
                    pe.wait_ge(s_prep, 3)
                in_pairs(pe, NB, body)
                logits(NB - 1, 1)

            def ranks(l):
                pe.wait_ge(L[l]["routed"], 1)
                oh = onehot[:].rearrange("p t e -> p (t e)")
                pe.matmul(bank[:, 4, :], before16[:], oh, start=True, stop=True)
                pe.matmul(bank[:, 5, :], ones16[:], oh, start=True, stop=True).then_inc(L[l]["rank"], 1)

            def attention():
                S = L[0]

                def t_of(b):
                    past(pe, S["v_lo"], b)
                    x = xnt(0, b)
                    product(bank[:, 7, :], lambda h: m16[:, h, :], lambda h: x[:, h, :]).then_inc(S["t_mm"], 1)

                def v_of(b):
                    pe.wait_ge(S["t_lo"], b + 1)
                    x = xnt(0, b)
                    for k in range(K):
                        m = product(bank[:, 7, k * D:k * D + D], lambda h: x[:, h, k * P:k * P + P],
                                    lambda h: wv16[:, h, :])
                    m.then_inc(S["v_mm"], 1)

                def scores(b, u, q, p):
                    pe.wait_ge(S["t_lo"], b + 1)
                    past(pe, S["expd"], u - 3)
                    x = xnt(0, b)
                    product(bank[:, q, :], lambda h: t16[:, p, h, q * P:q * P + P],
                            lambda h: x[:, h, :]).then_inc(S["score"], 1)

                def turn(u, q):
                    pe.wait_ge(S["expd"], u + 1)
                    past(pe, S["pt_lo"], u - 1)
                    for k in range(K):
                        m = pe.transpose(bank[:, 4 + q % 2, k * P:k * P + P], prob[:, q % 2, k * P:k * P + P],
                                         ident32[:])
                    m.then_inc(S["pt"], 1)

                def weigh(u, q, p):
                    pe.wait_ge(S["pt_lo"], u + 1)
                    past(pe, S["att"], u)
                    out = bank[:, 6, 0:D]
                    for k in range(K):
                        m = product(out, lambda h: pt16[:, q % 2, h, k, :], lambda h: v16[:, p, h, k, :],
                                    start=k == 0, stop=k == K - 1)
                    m.then_inc(S["pv"], 1)

                pe.wait_ge(s_prep, 6)
                pe.wait_ge(S["routed"], 3)
                t_of(0)
                v_of(0)
                scores(0, 0, 0, 0)
                scores(0, 1, 1, 0)

                def body(b, j, p):
                    for q in range(K):
                        u = K * b + q
                        if q == 0 and within(b + 1, NB):
                            t_of(b + 1)
                        if within(u + 2, NT):
                            if q < 2:
                                scores(b, u + 2, q + 2, p)
                            else:
                                scores(b + 1, u + 2, q - 2, 1 - p)
                        turn(u, q)
                        if q == 2 and within(b + 1, NB):
                            v_of(b + 1)
                        if within(u - 1, NT):
                            weigh(u - 1, (q + 3) % K, p if q else 1 - p)
                in_pairs(pe, NB, body)
                weigh(NT - 1, K - 1, 1)

            def linear_attention():
                S = LIN

                def qkv(b):
                    past(pe, S["qn"], b)
                    x = xnt(1, b)
                    for k in range(K):
                        m = product(bank[:, k, 0:3 * D], lambda h: x[:, h, k * P:k * P + P],
                                    lambda h: wqkv16[:, h, :])
                    m.then_inc(S["qkv"], 1)

                def state(b, p):
                    pe.wait_ge(S["sp"], b + 1)
                    past(pe, S["kvs"], b)
                    for k in range(K):
                        m = pe.matmul(bank[:, 4, 0:D + 2], sp[:, p, k, D:2 * D], v_one[:, p, k, :],
                                      start=k == 0, stop=k == K - 1)
                    m.then_inc(S["kv"], 1)
                    past(pe, S["qts"], b)
                    for k in range(K):
                        m = pe.transpose(bank[:, 5, k * P:k * P + P], sp[:, p, k, 0:D], ident32[:])
                    m.then_inc(S["qt"], 1)

                def read(b):
                    pe.wait_ge(S["kvs"], b + 1)
                    pe.wait_ge(S["qts"], b + 1)
                    past(pe, S["att"], b)
                    for k in range(K):
                        n = (k % 2) * (D + NH)
                        m = pe.matmul(bank[:, 6 + k // 2, n:n + D + NH], q_t[:, k * P:k * P + P], kvs[:],
                                      start=True, stop=True)
                    m.then_inc(S["out"], 1)

                def body(b, j, p):
                    qkv(b)
                    if within(b - 1, NB):
                        state(b - 1, 1 - p)
                        read(b - 1)
                pe.wait_ge(L[1]["routed"], 3)
                in_pairs(pe, NB, body)
                state(NB - 1, 1)
                read(NB - 1)

            def experts(l):
                S = L[l]

                def turn(s, j, r):
                    pe.wait_ge(S[f"ld{r}"], 16 * (j + 1))
                    past(pe, S["xg_s"], s - 1)
                    dst = bank[:, r % 2, 0:P].bitcast(F16).rearrange("p (h n) -> p h n", h=2)
                    for h in range(2):
                        m = pe.transpose(dst[:, h, :], xg[:, r, h, :], ident16[:])
                    m.then_inc(S["xg_t"], 1)

                def expert_of(s):
                    src = tile_expert[0:1, s:s + 1] if isinstance(s, int) else tile_expert[0:1, bass.ds(s, 1)]
                    return bass.ds(pe.value_load(src, min_val=0, max_val=E - 1), 1)

                def up(s, r):
                    e = expert_of(s)
                    pe.wait_ge(S["xg_s"], s + 1)
                    past(pe, S["h_lo"], s - 1)
                    for c in range(C):
                        out = bank[:, 2 + r % 2, c * P:c * P + P]
                        pe.matmul(out, bias16[:, e, c * P:c * P + P], ones16[:], start=True, stop=False)
                        m = product(out, lambda h: w1_16[:, e, h, c * P:c * P + P], lambda h: xgt[:, r % 2, h, :],
                                    start=False)
                    m.then_inc(S["up"], 1)

                def down(s, r):
                    e = expert_of(s)
                    pe.wait_ge(S["h_lo"], s + 1)
                    past(pe, S["y_v"], s - 1)
                    out = bank[:, 4 + r % 2, 0:D]
                    pe.matmul(out, ones16[:], bias16[:, e, FF:FF + D], start=True, stop=False)
                    for c in range(C):
                        m = product(out, lambda h: h16[:, r, h, c, :], lambda h: w2_16[:, e, h, c, :],
                                    start=False, stop=c == C - 1)
                    m.then_inc(S["down"], 1)

                def step(s, j, r):
                    if within(s, MT):
                        turn(s, j, r)
                    if within(s - 1, MT):
                        up(s - 1, (r + 3) % 4)
                    if within(s - 3, MT):
                        down(s - 3, (r + 1) % 4)

                pe.wait_ge(S["routed"], 3)
                pe.wait_ge(S["w_ready"], 6 * E)
                if l == 0:
                    pe.wait_ge(S["att"], NT)
                else:
                    pe.wait_ge(LIN["att"], NB)
                for s in range(8):
                    step(s, s // 4, s % 4)
                with pe.Fori(2, MT // 4) as j:
                    for r in range(4):
                        step(4 * j + r, j, r)
                for s in range(MT // 4 * 4, MT + 3):
                    step(s, s // 4, s % 4)

            norm_stage(0)
            ranks(0)
            attention()
            experts(0)
            norm_stage(1)
            ranks(1)
            linear_attention()
            experts(1)


_INS = ['L0_attn_x', 'L0_attn_Wq', 'L0_attn_Wk', 'L0_attn_Wv', 'L0_ffn_gate_w', 'L0_ffn_gate_b', 'L0_ffn_w1',
        'L0_ffn_b1', 'L0_ffn_w2', 'L0_ffn_b2', 'L1_attn_W_qkv', 'L1_ffn_router_W', 'L1_ffn_router_b', 'L1_ffn_W1',
        'L1_ffn_b1', 'L1_ffn_W2', 'L1_ffn_b2']


def kernel(**inputs):
    import numpy as _np
    import concourse.bacc as _bacc
    from concourse import mybir as _mybir
    from concourse.bass_utils import run_bass_kernel_spmd as _run

    nc = _bacc.Bacc("TRN2", target_bir_lowering=False, num_devices=1)
    arrays, args = {}, []
    for name in _INS:
        a = _np.ascontiguousarray(inputs[name])
        arrays[f"in_{name}"] = a
        args.append(nc.dram_tensor(f"in_{name}", a.shape, _mybir.dt.from_np(a.dtype), kind="ExternalInput").ap())
    shape = inputs['L0_attn_x'].shape
    args.append(nc.dram_tensor("out", shape, _mybir.dt.float32, kind="ExternalOutput").ap())
    build(nc, *args)
    r = _run(nc, [arrays], core_ids=[0])
    return r.results[0]["out"]
```

```python
from contextlib import ExitStack

import concourse.bass as bass
from concourse import mybir

P = 128
ALU = mybir.AluOpType
ACT = mybir.ActivationFunctionType
AX = mybir.AxisListType
F32 = mybir.dt.float32
F16 = mybir.dt.float16
I32 = mybir.dt.int32
U32 = mybir.dt.uint32

RSQRT_SEED = 0x5F3759DF
NEWTON = 3


def past(engine, sem, value):
    if not (isinstance(value, int) and value <= 0):
        engine.wait_ge(sem, value)


def in_pairs(engine, n, body):
    for p in range(2):
        body(p, 0, p)
    with engine.Fori(1, n // 2 - 1) as j:
        for p in range(2):
            body(2 * j + p, j, p)
    for p in range(2):
        body(n - 2 + p, n // 2 - 1, p)


def within(b, n):
    return not isinstance(b, int) or 0 <= b < n


def build(nc, x_d, wq_d, wk_d, wv_d, gate_w, gate_b, ew1, eb1, ew2, eb2, wqkv_d, router_w, router_b,
          fw1, fb1, fw2, fb2, out_d):
    NB, TB, D = x_d.shape
    E, _, FF = ew1.shape
    NH = 16
    DH = D // NH
    K = TB // P
    NT = NB * K
    NU = NB // 2
    KU = 2 * K
    KH = K // 2
    C = FF // P
    TS = 2 * P
    MT = NT * P // TS + E - 1
    SLOTS = MT * TS
    MTP = MT + 1
    LN_EPS, L2_EPS, K_EPS = 1e-5, 1e-12, 1e-6
    QK_SCALE = float(D) ** -0.5
    KV_SCALE = float(DH) ** -0.5
    assert D == P and K == 4 and NB % 4 == 0 and C == 4 and NU == E

    rows_d = [nc.dram_tensor(f"sorted_rows_{l}", (SLOTS, 2 * D), F16, kind="Internal").ap() for l in range(2)]
    y_d = [nc.dram_tensor(f"sorted_y_{l}", (SLOTS, D), F32, kind="Internal").ap() for l in range(2)]

    with ExitStack() as ctx:
        def sb(name, shape, dt):
            return ctx.enter_context(nc.sbuf_tensor(name, shape, dt))

        def sem(name):
            return ctx.enter_context(nc.semaphore(name))

        x_sb = sb("x_sb", [P, NT, D], F32)
        xn16 = sb("xn16", [P, NT, 2, D], F16)
        slots = sb("slots", [P, NB + 2, K * D], F32)
        w1_16 = sb("w1_16", [P, E, 2, FF], F16)
        w2_16 = sb("w2_16", [P, E, 2, C, D], F16)
        bias16 = sb("bias16", [P, E, FF + D], F16)
        w_in = sb("w_in", [P, 2, FF], F32)
        b_in = sb("b_in", [P, FF + D], F32)
        b_hi = sb("b_hi", [P, FF + D], F16)
        second_row = sb("second_row", [P, 1], F32)
        pool_carrier = sb("pool_carrier", [P, 2], F32)
        ident16 = sb("ident16", [P, P], F16)
        ident32 = sb("ident32", [P, P], F32)
        ones16 = sb("ones16", [P, TS], F16)
        before16 = sb("before16", [P, P], F16)
        headmask = sb("headmask", [P, P], F32)
        headcol = sb("headcol", [P, NH], F32)
        from_last = sb("from_last", [P, E], F32)
        tile_no = sb("tile_no", [P, MTP], F32)
        ring = sb("ring", [P, 2, K * D], F32)
        wsmall = ring[:, :, :].rearrange("p a n -> p (a n)")[:, 0:6 * D].rearrange("p (i n) -> p i n", i=6)
        m16 = sb("m16", [P, 2, D], F16)
        wv16 = sb("wv16", [P, 2, D], F16)
        wqkv16 = sb("wqkv16", [P, 2, 3 * D], F16)
        rw32 = sb("rw32", [P, 2, E], F32)
        rw16 = sb("rw16", [P, 2, 2, E], F16)
        rbias = sb("rbias", [P, 2, E], F32)
        work = sb("work", [P, 2, KU * D], F32)
        tanh = work[:, :, :].rearrange("p b (k d) -> p b k d", k=KU)
        stats = sb("stats", [P, 2, KU, 6], F32)
        mv = sb("mv", [P, 2, KU, 2], F32)
        nw_v = sb("nw_v", [P, 2, KU], F32)
        nw_y = sb("nw_y", [P, 2, KU], F32)
        nw_a = sb("nw_a", [P, 2, KU], F32)
        shift = sb("shift", [P, 2, KU], F32)
        lg = sb("lg", [P, NT, E], F32)
        best = sb("best", [P, NT], F32)
        carrier = sb("carrier", [P, 1], F32)
        expert = sb("expert", [P, NT], F32)
        halfgate = sb("halfgate", [P, NT], F32)
        onehot = sb("onehot", [P, NT, E], F16)
        small = sb("small", [P, 8, E], F32)
        smalli = sb("smalli", [P, 2, E], I32)
        tile_expert = sb("tile_expert", [P, MTP], I32)
        pos = sb("pos", [P, NT], U32)
        pos_io = sb("pos_io", [P, 2, KU], U32)
        row_io = sb("row_io", [P, K, D], U32)
        tv = sb("tv", [P, 4 * 2 * TB // 2], F32)
        t16 = tv[:, 0:2 * TB].bitcast(F16).rearrange("p (b h n) -> p b h n", b=2, h=2)
        xnf = tv[:, :].rearrange("p (b k d) -> p b k d", b=2, k=KU)
        v16 = tv[:, 2 * TB:4 * TB].bitcast(F16).rearrange("p (b h k n) -> p b h k n", b=2, h=2, k=K)
        prob = sb("prob", [P, 2, TB], F32)
        pt16 = sb("pt16", [P, 2, 2, K, P], F16)
        tot, incl = prob[:, 0, :], prob[:, 1, :]
        mask = prob[:, 0, :].rearrange("p (t e) -> p t e", e=E)
        cmp = pt16[:, :, :, :, :].rearrange("p a b k n -> p (a b k n)").bitcast(F32)[:, 0:MTP * E].rearrange(
            "p (t e) -> p t e", e=E)
        nmax = sb("nmax", [P, K], F32)
        rsum = sb("rsum", [P, K], F32)
        rden = sb("rden", [P, K], F32)
        qk_n = tv[:, :].rearrange("p (b k n) -> p b k n", b=2, k=K)
        sq = prob[:, :, :].rearrange("p a (k n) -> p a k n", k=KH)
        sp = work[:, :, :].rearrange("p b (k n) -> p b k n", k=K)
        v_one = sb("v_one", [P, 2, K, D + 2], F32)
        q_t = pt16[:, 0, :, :, :].rearrange("p b k n -> p (b k n)").bitcast(F32)
        kvs = sb("kvs", [P, D + NH], F32)
        ks = sb("ks", [P, 1], F32)
        ss = sb("ss", [P, 2, 3, KH * 2 * NH], F32)
        half30 = sb("half30", [P, 1], F32)
        rdn = sb("rdn", [P, K, NH], F32)
        xg = ring[:, 0, :].bitcast(F16).rearrange("p (s t h d) -> p s t h d", s=2, t=2, h=2)
        xgt = sb("xgt", [P, 2, 2, TS], F16)
        h32 = pt16[:, :, :, :, :].rearrange("p a b k n -> p (a b k n)").bitcast(F32).rearrange(
            "p (a n) -> p a n", a=2)
        h16 = sb("h16", [P, 2, 2, C, TS], F16)
        y_sb = ring[:, 1, :].rearrange("p (s t d) -> p s t d", s=2, t=2)
        y_back = h16[:, :, :, :, :].rearrange("p a b c n -> p (a b c n)").bitcast(F32).rearrange(
            "p (b k d) -> p b k d", b=2, k=KU)
        zrow = h16[:, :, :, :, :].rearrange("p a b c n -> p (a b c n)").bitcast(F32)[:, 0:SLOTS // P * D // 8]

        bank = ctx.enter_context(nc.psum_tensor("bank", [P, 8, 512], F32))

        s_const = sem("s_const")
        s_zero = sem("s_zero")
        s_zeroed = [sem(f"s_zeroed{l}") for l in range(2)]
        s_small = sem("s_small")
        s_x = [sem(f"s_x{p}") for p in range(2)]
        s_prep = sem("s_prep")
        s_prep_mm = sem("s_prep_mm")
        s_step = sem("s_step")
        s_out = [sem(f"s_out{p}") for p in range(2)]
        SUMMED = 3
        NORM_STEPS = [2 * KU + 3 + 3 * NEWTON, 2 * KU + 3 + 3 * NEWTON + SUMMED]
        FIN_STEPS = KU + 2
        NAMES = ["w1_in", "w2_in", "b_in", "w1_hi", "w2_hi", "b_hi", "w1_lo", "w2_lo", "b_lo", "rstd", "gathered", "gathered1", "tanh", "norm_step", "xn", "hi", "lo",
                 "xt", "xts", "logits", "lg",  "gate_e", "routed", "rank", "rows_out",
                 "staged", "scat0", "scat1", "scat2", "scat3",
                 "t_mm", "t_hi", "t_lo", "v_mm", "v_hi", "v_lo", "score", "rmax", "expd", "rcp", "pt", "pt_hi",
                 "pt_lo", "pv", "att",
                 "ld0", "ld1", "ld2", "ld3", "xg_t", "xg_s", "up", "h_hi", "h_lo", "down", "y_v",
                 "st0", "st1", "st2", "st3"]
        L = [{n: sem(f"{n}_{l}") for n in NAMES} for l in range(2)]
        LIN = {n: sem(f"lin_{n}") for n in ["qkv", "sq", "v", "step", "rstep", "rdn", "r0", "qn", "exp", "sp", "kv", "qt", "kvs",
                                            "qts", "out", "att"]}
        FIN = {n: sem(f"fin_{n}") for n in ["g0", "g1", "tanh", "step"]}

        def xnt(l, b):
            i = b + 2 - l
            v = slots[:, i:i + 1, :] if isinstance(i, int) else slots[:, bass.ds(i, 1), :]
            return v.bitcast(F16).rearrange("p o (h n) -> p (o h) n", h=2)

        def att(l, b):
            i = b + 1 - l
            v = slots[:, i:i + 1, :] if isinstance(i, int) else slots[:, bass.ds(i, 1), :]
            return v.rearrange("p o (k d) -> p (o k) d", k=K)

        def tiles(t, b):
            return t[:, bass.ds(K * b, K)] if not isinstance(b, int) else t[:, K * b:K * b + K]

        def unit(t, u):
            return t[:, bass.ds(KU * u, KU)] if not isinstance(u, int) else t[:, KU * u:KU * u + KU]

        def unit_slots(first, u):
            i = 2 * u + first
            return slots[:, i:i + 2, :] if isinstance(i, int) else slots[:, bass.ds(i, 2), :]

        def unit_att(l, u):
            return unit_slots(1 - l, u).rearrange("p o (k d) -> p (o k) d", k=K)

        def unit_rows(t, u):
            src = t[bass.ds(2 * u, 2)] if not isinstance(u, int) else t[2 * u:2 * u + 2]
            return src.rearrange("o (k p) d -> p (o k) d", p=P)

        block = ctx.enter_context(nc.Block())

        @block.sync
        def _(sp_):
            def load_x(u, j, p):
                past(sp_, s_x[p], 16 * j)
                sp_.dma_start(unit(x_sb, u), unit_rows(x_d, u)).then_inc(s_x[p], 16)

            def load_expert(l, e, w1, b1, w2, b2):
                def of(t):
                    return t[bass.ds(e, 1)] if not isinstance(e, int) else t[e:e + 1]
                S = L[l]
                past(sp_, S["w1_lo"], e)
                sp_.dma_start(w_in[:, 0, :], of(w1).rearrange("o d f -> d (o f)")).then_inc(S["w1_in"], 16)
                past(sp_, S["w2_lo"], e)
                sp_.dma_start(w_in[:, 1, :].rearrange("p (c d) -> p c d", c=C),
                              of(w2).rearrange("o (c p) d -> p (o c) d", p=P)).then_inc(S["w2_in"], 16)
                past(sp_, S["b_lo"], e)
                for r in (0, 32):
                    sp_.dma_start(b_in[r:r + 1, 0:FF], of(b1)).then_inc(S["b_in"], 16)
                    sp_.dma_start(b_in[r:r + 1, FF:FF + D], of(b2)).then_inc(S["b_in"], 16)

            def zero_rows(l):
                sp_.dma_start(rows_d[l].bitcast(F32).rearrange("(p a r) d -> p a (r d)", p=P, a=1).rearrange(
                    "p a (c n) -> p (a c) n", c=8),
                    zrow.unsqueeze(1).to_broadcast([P, 8, zrow.shape[1]])).then_inc(s_zeroed[l], 16)

            for u in range(2):
                load_x(u, 0, u)
            for i, w in enumerate((wq_d, wk_d, wv_d)):
                sp_.dma_start(wsmall[:, i, :], w).then_inc(s_small, 16)
            sp_.dma_start(wsmall[:, 3:6, :], wqkv_d.rearrange("(g o) d -> o g d", g=3)).then_inc(s_small, 16)
            for l, (w, b) in enumerate(((gate_w, gate_b), (router_w, router_b))):
                sp_.dma_start(rw32[:, l, :], w).then_inc(s_small, 16)
                sp_.dma_start(rbias[:, l, :], b.rearrange("(o e) -> o e", o=1).to_broadcast([P, E])).then_inc(s_small, 16)
            sp_.wait_ge(s_const, 1)
            weights = (ew1, eb1, ew2, eb2)
            load_expert(0, 0, *weights)
            load_x(2, 1, 0)
            load_expert(0, 1, *weights)
            sp_.wait_ge(s_zero, 1)
            zero_rows(0)
            with sp_.Fori(1, NU // 2 - 1) as j:
                for p in range(2):
                    load_x(2 * j + p + 1, j + p, 1 - p)
                    load_expert(0, 2 * j + p, *weights)
            load_x(NU - 1, NU // 2 - 1, 1)
            for e in range(E - 2, E):
                load_expert(0, e, *weights)
            zero_rows(1)

            def experts(l):
                def rows(t, s):
                    part = t[bass.ds(s * TS, TS)] if not isinstance(s, int) else t[s * TS:s * TS + TS]
                    return part.rearrange("(t p) n -> p t n", p=P)

                def step(s, j, r):
                    if within(s, MT):
                        past(sp_, L[l]["xg_t"], s - 1)
                        sp_.dma_start(xg[:, r % 2, :, :, :].rearrange("p t h d -> p t (h d)"),
                                      rows(rows_d[l], s)).then_inc(L[l][f"ld{r}"], 16)
                    if within(s - 4, MT):
                        sp_.wait_ge(L[l]["y_v"], s - 3)
                        sp_.dma_start(rows(y_d[l], s - 4), y_sb[:, r % 2, :, :]).then_inc(L[l][f"st{r}"], 16)
                for k in range(4):
                    sp_.wait_ge(L[l][f"scat{k}"], 16 * NB)
                for s in range(4):
                    step(s, 0, s)
                with sp_.Fori(1, MT // 4) as j:
                    for r in range(4):
                        step(4 * j + r, j, r)
                for s in range(MT // 4 * 4, MT + 4):
                    step(s, s // 4, s % 4)

            experts(0)
            load_expert(1, 0, fw1, fb1, fw2, fb2)
            with sp_.Fori(1, E) as e:
                load_expert(1, e, fw1, fb1, fw2, fb2)
            experts(1)

            def store(u, j, p):
                sp_.wait_ge(FIN["step"], FIN_STEPS * (u + 1))
                sp_.dma_start(unit_rows(out_d, u), unit(x_sb, u)).then_inc(s_out[p], 16)
            in_pairs(sp_, NU, store)
            for p in range(2):
                sp_.wait_ge(s_out[p], 16 * NU // 2)

        @block.gpsimd
        def _(pool):
            g = nc.gpsimd
            g.memset(pool_carrier[:], 0.0)
            g.memset(b_in[:], 0.0).then_inc(s_const, 1)
            g.memset(zrow, 0.0).then_inc(s_zero, 1)
            g.memset(ones16[:], 1.0).then_inc(s_const, 1)
            g.memset(second_row[:], 1.0).then_inc(s_const, 1)
            g.memset(ident32[:], 0.0).then_inc(s_const, 1)
            g.memset(headmask[:], KV_SCALE).then_inc(s_const, 1)
            g.memset(headcol[:], 1.0).then_inc(s_const, 1)
            g.memset(v_one[:], 1.0).then_inc(s_const, 1)
            g.iota(from_last[:], [[-1, E]], base=E, channel_multiplier=0,
                   allow_small_or_imprecise_dtypes=True).then_inc(s_const, 1)
            g.iota(tile_no[:], [[1, MTP]], base=0, channel_multiplier=0,
                   allow_small_or_imprecise_dtypes=True).then_inc(s_const, 1)
            pool.wait_ge(s_const, 9)
            g.affine_select(out=ident32[:], in_=ident32[:], compare_op=ALU.not_equal, fill=1.0, base=0,
                            pattern=[[-1, P]], channel_multiplier=1).then_inc(s_const, 1)
            g.affine_select(out=before16[:], in_=ones16[:, 0:P], compare_op=ALU.is_gt, fill=0.0, base=0,
                            pattern=[[1, P]], channel_multiplier=-1).then_inc(s_const, 1)
            hm = headmask[:, :].rearrange("p (h d) -> p h d", h=NH)
            g.affine_select(out=hm, in_=hm, compare_op=ALU.is_ge, fill=0.0, base=0,
                            pattern=[[-DH, NH], [0, DH]], channel_multiplier=1).then_inc(s_const, 1)
            g.affine_select(out=headcol[:], in_=headcol[:], compare_op=ALU.is_ge, fill=0.0, base=0,
                            pattern=[[-DH, NH]], channel_multiplier=1).then_inc(s_const, 1)
            g.affine_select(out=second_row[:], in_=second_row[:], compare_op=ALU.is_ge, fill=0.0, base=-32,
                            pattern=[[0, 1]], channel_multiplier=1).then_inc(s_const, 1)
            pool.wait_ge(s_const, 14)
            g.affine_select(out=hm, in_=hm, compare_op=ALU.is_ge, fill=0.0, base=DH - 1,
                            pattern=[[DH, NH], [0, DH]], channel_multiplier=-1).then_inc(s_const, 1)
            g.affine_select(out=headcol[:], in_=headcol[:], compare_op=ALU.is_ge, fill=0.0, base=DH - 1,
                            pattern=[[DH, NH]], channel_multiplier=-1).then_inc(s_const, 1)
            g.tensor_copy(ident16[:], ident32[:]).then_inc(s_const, 1)

            def carry():
                g.tensor_tensor(pool_carrier[:, 1:2], pool_carrier[:, 0:1], pool_carrier[:, 0:1], ALU.add)

            def weights_low(l, e):
                def of(t):
                    return t[:, bass.ds(e, 1)] if not isinstance(e, int) else t[:, e:e + 1]
                S = L[l]
                w1o, bo = of(w1_16), of(bias16)
                w2o = of(w2_16).rearrange("p o h c d -> p o h (c d)")
                pool.wait_ge(S["w1_hi"], e + 1)
                g.tensor_tensor(w1o[:, :, 1, :], w_in[:, 0:1, :], w1o[:, :, 0, :], ALU.subtract).then_inc(S["w1_lo"], 1)
                pool.wait_ge(S["w2_hi"], e + 1)
                g.tensor_tensor(w2o[:, :, 1, :], w_in[:, 1:2, :], w2o[:, :, 0, :], ALU.subtract).then_inc(S["w2_lo"], 1)
                pool.wait_ge(S["b_hi"], e + 1)
                g.tensor_tensor(bo, b_in[:, :].unsqueeze(1), b_hi[:, :].unsqueeze(1), ALU.subtract).then_inc(
                    S["b_lo"], 1)

            def fetch(u, j, p, ysrc, done, freed, per, at):
                past(pool, freed, per * (u - 2) + at)
                g.tensor_copy(pos_io[:, p, :], unit(pos, u)).then_inc(s_posio[0], 1)
                pool.wait_ge(s_posio[0], s_posio[1] + u + 1)
                carry()
                for k in range(KU):
                    g.indirect_dma_start(y_back[:, p, k, :], None, ysrc[:, :],
                                         bass.IndirectOffsetOnAxis(pos_io[:, p, k:k + 1], 0)).then_inc(done[p], 16)

            def norm_stage(l):
                def body(u, j, p):
                    if l == 1:
                        if isinstance(u, int) and u == 0:
                            for uu in range(2):
                                fetch(uu, 0, uu, y_d[0], [L[1]["gathered"], L[1]["gathered1"]], L[1]["norm_step"],
                                      NORM_STEPS[1], SUMMED)
                        if within(u + 2, NU):
                            fetch(u + 2, j + 1, p, y_d[0], [L[1]["gathered"], L[1]["gathered1"]], L[1]["norm_step"],
                                  NORM_STEPS[1], SUMMED)
                    pool.wait_ge(L[l]["hi"], u + 1)
                    hl = unit(xn16, u)
                    g.tensor_tensor(hl[:, :, 1, :], xnf[:, p, :, :], hl[:, :, 0, :], ALU.subtract).then_inc(
                        L[l]["lo"], 1)
                    weights_low(l, u)
                in_pairs(pool, NU, body)

            def scatter(l):
                pool.wait_ge(L[l]["routed"], 2)
                pool.wait_ge(s_zeroed[l], 16)

                def body(b, first):
                    for k in range(K):
                        if not first:
                            pool.wait_ge(L[l][f"scat{k}"], 16 * b)
                    st = L[l]["staged"]
                    g.tensor_copy(pos_io[:, 0, 0:K], tiles(pos, b)).then_inc(st, 1)
                    g.tensor_copy(row_io[:, :, :], tiles(xn16, b).rearrange("p k h d -> p k (h d)").bitcast(U32)
                                  ).then_inc(st, 1)
                    pool.wait_ge(st, 2 * b + 2)
                    carry()
                    for k in range(K):
                        g.indirect_dma_start(rows_d[l][:, :], bass.IndirectOffsetOnAxis(pos_io[:, 0, k:k + 1], 0),
                                             row_io[:, k, :].bitcast(F16), None).then_inc(L[l][f"scat{k}"], 16)
                body(0, True)
                with pool.Fori(1, NB) as b:
                    body(b, False)

            s_posio = [sem("s_posio_a"), 0]
            norm_stage(0)
            scatter(0)
            for r in range(4):
                pool.wait_ge(L[0][f"st{r}"], 16 * len(range(r, MT, 4)))
            norm_stage(1)
            scatter(1)
            for r in range(4):
                pool.wait_ge(L[1][f"st{r}"], 16 * len(range(r, MT, 4)))
            s_posio = [sem("s_posio_b"), 0]
            for bb in range(2):
                fetch(bb, 0, bb, y_d[1], [FIN["g0"], FIN["g1"]], FIN["step"], FIN_STEPS, 1)
            with pool.Fori(1, NU // 2) as j:
                for p in range(2):
                    fetch(2 * j + p, j, p, y_d[1], [FIN["g0"], FIN["g1"]], FIN["step"], FIN_STEPS, 1)

        @block.scalar
        def _(act):
            a = nc.scalar

            def norm_stage(l):
                S = L[l]

                def t_hyp(u, j, p):
                    act.wait_ge(S["gathered1" if p else "gathered"], 16 * KU * (j + 1))
                    past(act, S["norm_step"], NORM_STEPS[1] * (u - 2) + SUMMED)
                    a.activation(tanh[:, p, :, :], y_back[:, p, :, :], ACT.Tanh).then_inc(S["tanh"], 1)

                def weights_high(e):
                    def of(t):
                        return t[:, bass.ds(e, 1)] if not isinstance(e, int) else t[:, e:e + 1]
                    act.wait_ge(S["w1_in"], 16 * (e + 1))
                    a.activation(of(w1_16)[:, :, 0, :], w_in[:, 0:1, :], ACT.Copy).then_inc(S["w1_hi"], 1)
                    act.wait_ge(S["w2_in"], 16 * (e + 1))
                    a.activation(of(w2_16).rearrange("p o h c d -> p o h (c d)")[:, :, 0, :], w_in[:, 1:2, :],
                                 ACT.Copy).then_inc(S["w2_hi"], 1)
                    act.wait_ge(S["b_in"], 64 * (e + 1))
                    past(act, S["b_lo"], e)
                    a.activation(b_hi[:], b_in[:], ACT.Copy, scale=second_row[:, 0:1]).then_inc(S["b_hi"], 1)

                def body(u, j, p):
                    if l == 1:
                        if isinstance(u, int) and u == 0:
                            t_hyp(0, 0, 0)
                        if within(u + 1, NU):
                            t_hyp(u + 1, j + p, 1 - p)
                    act.wait_ge(S["rstd"], u + 1)
                    past(act, S["lo"], u - 1)
                    x = unit(x_sb, u)
                    for k in range(KU):
                        a.activation(xnf[:, p, k, :], x[:, k, :], ACT.Identity, scale=nw_y[:, p, k:k + 1],
                                     bias=shift[:, p, k:k + 1]).then_inc(S["xn"], 1)
                    act.wait_ge(S["xn"], KU * (u + 1))
                    hl = unit(xn16, u)
                    a.activation(hl[:, :, 0, :], xnf[:, p, :, :], ACT.Copy).then_inc(S["hi"], 1)
                    if within(u - 1, NU):
                        to_sbuf(u - 1, 1 - p)
                    weights_high(u)

                def to_sbuf(u, p):
                    act.wait_ge(S["xt"], u + 1)
                    a.activation(unit_slots(2 - l, u).bitcast(F16), bank[:, 2 * p:2 * p + 2, :].bitcast(F16),
                                 ACT.Copy).then_inc(S["xts"], 1)

                if l == 0:
                    act.wait_ge(s_const, 14)
                in_pairs(act, NU, body)
                to_sbuf(NU - 1, 1)
                if l == 1:
                    act.wait_ge(S["lg"], NU + 1)
                    a.activation(lg[:], lg[:], ACT.Exp).then_inc(S["gate_e"], 1)

            def attention():
                S = L[0]

                def t_high(b, p):
                    act.wait_ge(S["t_mm"], b + 1)
                    a.activation(t16[:, p, 0, :], bank[:, 7, :], ACT.Copy).then_inc(S["t_hi"], 1)

                def v_high(b, p):
                    act.wait_ge(S["v_mm"], b + 1)
                    a.activation(v16[:, p, 0, :, :], bank[:, 7, :].rearrange("p (k d) -> p k d", k=K),
                                 ACT.Copy).then_inc(S["v_hi"], 1)

                def softmax_exp(u, q):
                    act.wait_ge(S["rmax"], u + 1)
                    past(act, S["pt"], u - 1)
                    a.activation(prob[:, q % 2, :], bank[:, q, :], ACT.Exp, bias=nmax[:, q:q + 1],
                                 accum_out=rsum[:, q:q + 1]).then_inc(S["expd"], 1)

                def result(b, u, q):
                    act.wait_ge(S["rcp"], u + 1)
                    act.wait_ge(S["pv"], u + 1)
                    a.activation(att(0, b)[:, q, :], bank[:, 6, 0:D], ACT.Copy,
                                 scale=rden[:, q:q + 1]).then_inc(S["att"], 1)

                t_high(0, 0)
                v_high(0, 0)
                softmax_exp(0, 0)

                def body(b, j, p):
                    for q in range(K):
                        u = K * b + q
                        if q == 0 and within(b + 1, NB):
                            t_high(b + 1, 1 - p)
                        if q == 2 and within(b + 1, NB):
                            v_high(b + 1, 1 - p)
                        if within(u - 2, NT):
                            result(b if q >= 2 else b - 1, u - 2, (q + 2) % K)
                        if within(u + 1, NT):
                            softmax_exp(u + 1, (q + 1) % K)
                        act.wait_ge(S["pt"], u + 1)
                        past(act, S["pv"], u - 1)
                        a.activation(pt16[:, q % 2, 0, :, :],
                                     bank[:, 4 + q % 2, :].rearrange("p (k n) -> p k n", k=K),
                                     ACT.Copy).then_inc(S["pt_hi"], 1)
                in_pairs(act, NB, body)
                result(NB - 1, NT - 2, 2)
                result(NB - 1, NT - 1, 3)

            def linear_attention():
                S = LIN

                def front(b, i, p):
                    h = 2 * b + i
                    act.wait_ge(S["qkv"], h + 1)
                    qkv = bank[:, KH * i:KH * i + KH, :]
                    past(act, S["step"], 5 * (h - 2) + 1)
                    a.activation(sq[:, i, :, :], qkv[:, :, 0:2 * D], ACT.Square).then_inc(S["sq"], 1)
                    past(act, S["kv"], b - 1)
                    a.activation(v_one[:, p, KH * i:KH * i + KH, 0:D], qkv[:, :, 2 * D:3 * D],
                                 ACT.Copy).then_inc(S["v"], 1)

                def inv_norm(b, i):
                    h = 2 * b + i
                    r = ss[:, i, 1, :]
                    act.wait_ge(S["step"], 5 * h + 2)
                    a.activation(r, ss[:, i, 0, :], ACT.Ln, scale=2.0 ** 30).then_inc(S["r0"], 1)
                    act.wait_ge(S["r0"], 2 * h + 1)
                    a.activation(r, r, ACT.Exp, scale=-0.5, bias=half30[:, 0:1]).then_inc(S["r0"], 1)

                def softplus(b, i, p):
                    h = 2 * b + i
                    act.wait_ge(S["qn"], h + 1)
                    x = qk_n[:, p, KH * i:KH * i + KH, :]
                    a.activation(x, x, ACT.Exp).then_inc(S["exp"], 1)
                    act.wait_ge(S["exp"], h + 1)
                    past(act, S["kv"], b - 1)
                    past(act, S["qt"], b - 1)
                    a.activation(sp[:, p, KH * i:KH * i + KH, :], x, ACT.Ln, bias=1.0).then_inc(S["sp"], 1)

                def q_out(b):
                    act.wait_ge(S["qt"], b + 1)
                    past(act, S["out"], b)
                    a.activation(q_t[:, :], bank[:, 5, :], ACT.Copy).then_inc(S["qts"], 1)

                def body(b, j, p):
                    for i in range(2):
                        if within(b, NB):
                            front(b, i, p)
                        if i == 0 and within(b - 1, NB):
                            softplus(b - 1, 1, 1 - p)
                        if i == 1 and within(b, NB):
                            softplus(b, 0, p)
                        if within(b, NB):
                            inv_norm(b, i)
                        if i == 1 and within(b - 1, NB):
                            q_out(b - 1)
                nc.scalar.preload_act_table_set("natural_log_exp_and_others")
                in_pairs(act, NB, body)
                body(NB, 0, 0)

            def experts(l):
                S = L[l]

                def step(u, r):
                    for g in range(2):
                        act.wait_ge(S["up"], 2 * u + g + 1)
                        past(act, S["down"], u - 1)
                        h = bank[:, 2 + 2 * (r % 2) + g, :].rearrange("p (c n) -> p c n", c=C // 2)
                        f = ACT.Gelu if l == 0 else ACT.Relu
                        a.activation(h16[:, r % 2, 0, 2 * g:2 * g + 2, :], h, f).then_inc(S["h_hi"], 1)
                        if l == 0:
                            past(act, S["h_lo"], 2 * u - 1 + g)
                            a.activation(h32[:, g, :].rearrange("p (c n) -> p c n", c=C // 2), h,
                                         f).then_inc(S["h_hi"], 1)
                if l == 0:
                    for zeroed in s_zeroed:
                        act.wait_ge(zeroed, 16)
                for u in range(4):
                    step(u, u)
                with act.Fori(1, MT // 4) as j:
                    for r in range(4):
                        step(4 * j + r, r)
                for u in range(MT // 4 * 4, MT):
                    step(u, u % 4)

            def final():
                def body(u, j, p):
                    act.wait_ge(FIN["g1" if p else "g0"], 16 * KU * (j + 1))
                    past(act, FIN["step"], FIN_STEPS * (u - 2) + FIN_STEPS)
                    hg = unit(halfgate, u)
                    for k in range(KU):
                        a.activation(tanh[:, p, k, :], y_back[:, p, k, :], ACT.Tanh,
                                     scale=hg[:, k:k + 1]).then_inc(FIN["tanh"], 1)
                in_pairs(act, NU, body)

            norm_stage(0)
            attention()
            experts(0)
            norm_stage(1)
            linear_attention()
            experts(1)
            final()

        @block.vector
        def _(dve):
            v = nc.vector
            count = [0]

            def link(ins):
                count[0] += 1
                ins.then_inc(s_step, 1)
                dve.wait_ge(s_step, count[0])

            def pair(dst, src):
                link(v.tensor_copy(dst[:, 0], src))
                v.tensor_tensor(dst[:, 1], src, dst[:, 0], ALU.subtract).then_inc(s_prep, 1)

            v.memset(half30[:], 15.0 * 0.6931471805599453).then_inc(s_prep, 1)
            dve.wait_ge(s_small, 16 * 8)
            for l in range(2):
                pair(rw16[:, l], rw32[:, l, :])
            dve.wait_ge(s_prep_mm, 1)
            link(v.tensor_scalar(wsmall[:, 0, :], bank[:, 4, 0:D], QK_SCALE, None, ALU.mult))
            pair(m16, wsmall[:, 0, :])
            dve.wait_ge(s_prep_mm, 2)
            pair(wv16, bank[:, 5, 0:D])
            dve.wait_ge(s_prep_mm, 3)
            pair(wqkv16, bank[:, 6, 0:3 * D])

            def norm_stage(l):
                S = L[l]
                STEPS = NORM_STEPS[l]

                def body(u, j, p):
                    n = [0]

                    def step(ins, wait=True):
                        n[0] += 1
                        ins.then_inc(S["norm_step"], 1)
                        if wait:
                            dve.wait_ge(S["norm_step"], STEPS * u + n[0])

                    x = unit(x_sb, u)
                    if l == 0:
                        dve.wait_ge(s_x[p], 16 * (j + 1))
                    else:
                        dve.wait_ge(S["tanh"], u + 1)
                        t = tanh[:, p, :, :]
                        step(v.scalar_tensor_tensor(out=t, in0=t, scalar=1.0, in1=y_back[:, p, :, :],
                                                    op0=ALU.add, op1=ALU.mult))
                        step(v.tensor_tensor(t, t, unit_att(0, u), ALU.mult))
                        step(v.tensor_tensor(x, x, t, ALU.add))
                    v.memset(carrier[:], 0.0)
                    for k in range(KU):
                        step(v.bn_stats(stats[:, p, k, :], x[:, k, :]), wait=k == KU - 1)
                    v.memset(carrier[:], 0.0)
                    for k in range(KU):
                        step(v.bn_aggr(mv[:, p, k, :], stats[:, p, k, :]), wait=k == KU - 1)
                    vv, y, w = nw_v[:, p, :], nw_y[:, p, :], nw_a[:, p, :]
                    past(dve, S["xn"], KU * (u - 1))
                    step(v.tensor_scalar(vv, mv[:, p, :, 1], LN_EPS, None, ALU.add))
                    step(v.tensor_scalar(w.bitcast(I32), vv.bitcast(I32), 1, None, ALU.arith_shift_right))
                    step(v.tensor_scalar(y.bitcast(I32), w.bitcast(I32), -1.0, float(RSQRT_SEED), ALU.mult, ALU.add))
                    for _ in range(NEWTON):
                        step(v.tensor_tensor(w, y, y, ALU.mult))
                        step(v.scalar_tensor_tensor(out=w, in0=w, scalar=-0.5, in1=vv, op0=ALU.mult, op1=ALU.mult))
                        step(v.scalar_tensor_tensor(out=y, in0=w, scalar=1.5, in1=y, op0=ALU.add, op1=ALU.mult))
                    v.scalar_tensor_tensor(out=shift[:, p, :], in0=mv[:, p, :, 0], scalar=-1.0, in1=y,
                                           op0=ALU.mult, op1=ALU.mult).then_inc(S["rstd"], 1)
                    assert n[0] == STEPS
                    if within(u - 2, NU):
                        keep_logits(u - 2, p)

                def keep_logits(u, p):
                    dve.wait_ge(S["logits"], u + 1)
                    v.tensor_tensor(unit(lg, u), bank[:, 4 + p, 0:KU * E].rearrange("p (k e) -> p k e", k=KU),
                                    rbias[:, l, :].unsqueeze(1).to_broadcast([P, KU, E]), ALU.add).then_inc(S["lg"], 1)

                in_pairs(dve, NU, body)
                keep_logits(NU - 2, 0)
                keep_logits(NU - 1, 1)

            def routing(l):
                S = L[l]
                dve.wait_ge(S["lg"], NU)
                wide = [P, NT, E]

                def spread(t):
                    return t.unsqueeze(2).to_broadcast(wide)

                def top(values):
                    link(v.tensor_reduce(best[:], values, AX.X, ALU.max))
                    link(v.tensor_tensor(mask, values, spread(best[:]), ALU.is_equal))
                    link(v.tensor_tensor(mask, mask, from_last[:].unsqueeze(1).to_broadcast(wide), ALU.mult))

                top(lg[:])
                link(v.tensor_reduce(expert[:], mask, AX.X, ALU.max))
                if l == 0:
                    link(v.tensor_tensor(mask, from_last[:].unsqueeze(1).to_broadcast(wide), spread(expert[:]),
                                         ALU.is_equal))
                    link(v.scalar_tensor_tensor(out=lg[:], in0=mask, scalar=-3.0e38, in1=lg[:], op0=ALU.mult,
                                                op1=ALU.add))
                    top(lg[:])
                    link(v.tensor_reduce(best[:], mask, AX.X, ALU.max))
                    link(v.tensor_tensor(expert[:], expert[:], best[:], ALU.min))
                else:
                    v.tensor_tensor(lg[:], lg[:], spread(best[:]), ALU.subtract).then_inc(S["lg"], 1)
                v.tensor_tensor(onehot[:], expert[:].unsqueeze(2).to_broadcast([P, NT, E]),
                                from_last[:].unsqueeze(1).to_broadcast([P, NT, E]), ALU.is_equal).then_inc(S["routed"], 1)
                dve.wait_ge(S["rank"], 1)
                by_expert = tot.rearrange("p (e t) -> p t e", e=E)
                link(v.tensor_copy(by_expert, bank[:, 5, :].rearrange("p (t e) -> p t e", e=E)))
                link(v.tensor_tensor_scan(incl, tot, tot, 0.0, ALU.add, ALU.max))
                inc_v = incl.rearrange("p (e t) -> p e t", e=E)
                ends = inc_v[:, :, NT - 1]
                start, n, nt, tc, delta = (small[:, i, :] for i in range(5))
                link(v.memset(start, 0.0))
                link(v.tensor_copy(start[:, 1:E], ends[:, 0:E - 1]))
                link(v.tensor_tensor(n, ends, start, ALU.subtract))
                link(v.tensor_scalar(smalli[:, 0, :], n, float(TS - 1), None, ALU.add))
                link(v.tensor_scalar(smalli[:, 1, :], smalli[:, 0, :], TS.bit_length() - 1, None, ALU.arith_shift_right))
                link(v.tensor_copy(nt, smalli[:, 1, :]))
                link(v.tensor_tensor_scan(tc, nt, nt, 0.0, ALU.add, ALU.max))
                link(v.tensor_tensor(delta, tc, nt, ALU.subtract))
                link(v.scalar_tensor_tensor(out=delta, in0=delta, scalar=float(TS), in1=start, op0=ALU.mult,
                                            op1=ALU.subtract))
                link(v.tensor_tensor(incl, incl, tot, ALU.subtract))
                link(v.tensor_tensor(inc_v, inc_v, delta.unsqueeze(2).to_broadcast([P, E, NT]), ALU.add))
                te = incl.rearrange("p (e t) -> p t e", e=E)
                tt = tot.rearrange("p (t e) -> p t e", e=E)
                link(v.tensor_tensor(tt, te, bank[:, 4, :].rearrange("p (t e) -> p t e", e=E), ALU.add))
                link(v.tensor_tensor(tt, tt, onehot[:], ALU.mult))
                with nc.allow_low_precision(reason="whole numbers below 2^24, summed in float32"):
                    v.tensor_reduce(pos[:], tt, AX.X, ALU.add).then_inc(S["routed"], 1)
                link(v.tensor_tensor(cmp, tile_no[:].unsqueeze(2).to_broadcast([P, MTP, E]),
                                     tc.unsqueeze(1).to_broadcast([P, MTP, E]), ALU.is_ge))
                link(v.tensor_reduce(incl[:, 0:MTP], cmp, AX.X, ALU.add))
                v.tensor_scalar(tile_expert[:], incl[:, 0:MTP], float(E - 1), None, ALU.min).then_inc(S["routed"], 1)
                if l == 1:
                    dve.wait_ge(S["gate_e"], 1)
                    link(v.tensor_reduce(halfgate[:], lg[:], AX.X, ALU.add))
                    link(v.reciprocal(halfgate[:], halfgate[:]))
                    link(v.tensor_scalar(halfgate[:], halfgate[:], 0.5, None, ALU.mult))

            def attention():
                S = L[0]

                def t_low(b, p):
                    dve.wait_ge(S["t_hi"], b + 1)
                    v.tensor_tensor(t16[:, p, 1, :], bank[:, 7, :], t16[:, p, 0, :], ALU.subtract).then_inc(S["t_lo"], 1)

                def v_low(b, p):
                    dve.wait_ge(S["v_hi"], b + 1)
                    v.tensor_tensor(v16[:, p, 1, :, :], bank[:, 7, :].rearrange("p (k d) -> p k d", k=K),
                                    v16[:, p, 0, :, :], ALU.subtract).then_inc(S["v_lo"], 1)

                def row_max(u, q):
                    dve.wait_ge(S["score"], u + 1)
                    past(dve, S["expd"], u - 3)
                    v.tensor_reduce(nmax[:, q:q + 1], bank[:, q, :], AX.X, ALU.max, negate=True).then_inc(S["rmax"], 1)

                t_low(0, 0)
                v_low(0, 0)
                row_max(0, 0)
                row_max(1, 1)

                def body(b, j, p):
                    for q in range(K):
                        u = K * b + q
                        if within(u + 2, NT):
                            row_max(u + 2, (q + 2) % K)
                        if q == 0 and within(b + 1, NB):
                            t_low(b + 1, 1 - p)
                        if q == 2 and within(b + 1, NB):
                            v_low(b + 1, 1 - p)
                        dve.wait_ge(S["expd"], u + 1)
                        past(dve, S["att"], u - 3)
                        v.reciprocal(rden[:, q:q + 1], rsum[:, q:q + 1]).then_inc(S["rcp"], 1)
                        dve.wait_ge(S["pt_hi"], u + 1)
                        v.tensor_tensor(pt16[:, q % 2, 1, :, :],
                                        bank[:, 4 + q % 2, :].rearrange("p (k n) -> p k n", k=K),
                                        pt16[:, q % 2, 0, :, :], ALU.subtract).then_inc(S["pt_lo"], 1)
                in_pairs(dve, NB, body)

            def linear_attention():
                S = LIN
                st = S["step"]

                def front(b, i):
                    h = 2 * b + i
                    dve.wait_ge(S["sq"], h + 1)
                    norm2 = ss[:, i, 0, :]
                    v.tensor_reduce(norm2.rearrange("p (k h) -> p k h", k=KH),
                                    sq[:, i, :, :].rearrange("p k (h d) -> p k h d", d=DH), AX.X, ALU.add
                                    ).then_inc(st, 1)
                    dve.wait_ge(st, 5 * h + 1)
                    v.tensor_scalar(norm2, norm2, L2_EPS * L2_EPS, None, ALU.max).then_inc(st, 1)

                def normalise(b, i, p):
                    h = 2 * b + i
                    norm2, r, w = (ss[:, i, n, :] for n in range(3))
                    dve.wait_ge(S["r0"], 2 * h + 2)
                    v.tensor_tensor(w, r, r, ALU.mult).then_inc(st, 1)
                    dve.wait_ge(st, 5 * h + 3)
                    v.scalar_tensor_tensor(out=w, in0=w, scalar=-0.5, in1=norm2, op0=ALU.mult,
                                           op1=ALU.mult).then_inc(st, 1)
                    dve.wait_ge(st, 5 * h + 4)
                    v.scalar_tensor_tensor(out=r, in0=w, scalar=1.5, in1=r, op0=ALU.add, op1=ALU.mult).then_inc(st, 1)
                    dve.wait_ge(st, 5 * h + 5)
                    dve.wait_ge(S["v"], h + 1)
                    rr = r.rearrange("p (k h) -> p k h", k=KH)
                    for n in range(KH):
                        k = KH * i + n
                        ins = v.tensor_tensor(qk_n[:, p, k, :].rearrange("p (h d) -> p h d", d=DH),
                                              bank[:, k, 0:2 * D].rearrange("p (h d) -> p h d", d=DH),
                                              rr[:, n, :].unsqueeze(2).to_broadcast([P, 2 * NH, DH]), ALU.mult)
                    ins.then_inc(S["qn"], 1)

                def state(b):
                    dve.wait_ge(S["kv"], b + 1)
                    past(dve, S["out"], b)
                    rs = S["rstep"]
                    v.tensor_scalar(ks[:], bank[:, 4, D:D + 1], K_EPS, None, ALU.add).then_inc(rs, 1)
                    v.tensor_tensor(kvs[:, 0:D], bank[:, 4, 0:D], headmask[:], ALU.mult).then_inc(rs, 1)
                    dve.wait_ge(rs, 2 * b + 2)
                    v.tensor_scalar(kvs[:, D:D + NH], headcol[:], ks[:, 0:1], None, ALU.mult).then_inc(S["kvs"], 1)

                def result(b):
                    dve.wait_ge(S["out"], b + 1)
                    rd = S["rdn"]
                    o = bank[:, 6:8, 0:2 * (D + NH)].rearrange("p a (k n) -> p a k n", k=2)
                    for i in range(2):
                        v.reciprocal(rdn[:, 2 * i:2 * i + 2, :], o[:, i, :, D:D + NH]).then_inc(rd, 1)
                    dve.wait_ge(rd, 2 * b + 2)
                    dst = att(1, b)
                    for k in range(K):
                        ins = v.tensor_tensor(dst[:, k, :].rearrange("p (h d) -> p h d", d=DH),
                                              o[:, k // 2, k % 2, 0:D].rearrange("p (h d) -> p h d", d=DH),
                                              rdn[:, k, :].unsqueeze(2).to_broadcast([P, NH, DH]), ALU.mult)
                    ins.then_inc(S["att"], 1)

                def body(b, j, p):
                    for i in range(2):
                        if within(b, NB):
                            front(b, i)
                        if i == 0 and within(b - 2, NB):
                            result(b - 2)
                        if i == 1 and within(b - 1, NB):
                            state(b - 1)
                        if within(b, NB):
                            normalise(b, i, p)
                in_pairs(dve, NB, body)
                body(NB, 0, 0)
                result(NB - 1)

            def experts(l):
                S = L[l]

                def step(s, j, r):
                    if within(s, MT):
                        dve.wait_ge(S["xg_t"], s + 1)
                        past(dve, S["up"], 2 * s - 2)
                        v.tensor_copy(xgt[:, r % 2, :, :],
                                      bank[:, r % 2, 0:TS].bitcast(F16).rearrange("p (h n) -> p h n", h=2)
                                      ).then_inc(S["xg_s"], 1)
                    if within(s - 1, MT):
                        u, ru = s - 1, (r + 1) % 2
                        for g in range(2):
                            chunks = slice(2 * g, 2 * g + 2)
                            if l == 0:
                                dve.wait_ge(S["h_hi"], 4 * u + 2 * g + 2)
                                v.tensor_tensor(h16[:, ru, 1, chunks, :],
                                                h32[:, g, :].rearrange("p (c n) -> p c n", c=C // 2),
                                                h16[:, ru, 0, chunks, :], ALU.subtract).then_inc(S["h_lo"], 1)
                            else:
                                h = bank[:, 2 + 2 * ru + g, :].rearrange("p (c n) -> p c n", c=C // 2)
                                dve.wait_ge(S["h_hi"], 2 * u + g + 1)
                                v.scalar_tensor_tensor(out=h16[:, ru, 1, chunks, :], in0=h, scalar=0.0,
                                                       in1=h16[:, ru, 0, chunks, :],
                                                       op0=ALU.max, op1=ALU.subtract).then_inc(S["h_lo"], 1)
                    if within(s - 2, MT):
                        dve.wait_ge(S["down"], s - 1)
                        past(dve, S[f"st{r}"], 16 * j)
                        v.tensor_copy(y_sb[:, r % 2, :, :].rearrange("p t d -> p (t d)"),
                                      bank[:, 6 + r % 2, 0:2 * D]).then_inc(S["y_v"], 1)
                for s in range(4):
                    step(s, 0, s)
                with dve.Fori(1, MT // 4) as j:
                    for r in range(4):
                        step(4 * j + r, j, r)
                for s in range(MT // 4 * 4, MT + 2):
                    step(s, s // 4, s % 4)

            def final():
                def body(u, j, p):
                    dve.wait_ge(FIN["tanh"], KU * (u + 1))
                    t = tanh[:, p, :, :]
                    st = FIN["step"]
                    N = FIN_STEPS
                    v.scalar_tensor_tensor(out=t, in0=t, scalar=1.0, in1=y_back[:, p, :, :],
                                           op0=ALU.add, op1=ALU.mult).then_inc(st, 1)
                    dve.wait_ge(st, N * u + 1)
                    hg, s1, x = unit(halfgate, u), unit_att(1, u), unit(x_sb, u)
                    for k in range(KU):
                        v.scalar_tensor_tensor(out=t[:, k, :], in0=t[:, k, :], scalar=hg[:, k:k + 1], in1=s1[:, k, :],
                                               op0=ALU.mult, op1=ALU.mult).then_inc(st, 1)
                    dve.wait_ge(st, N * u + 1 + KU)
                    v.tensor_tensor(x, x, t, ALU.add).then_inc(st, 1)
                in_pairs(dve, NU, body)

            norm_stage(0)
            routing(0)
            attention()
            experts(0)
            norm_stage(1)
            routing(1)
            linear_attention()
            experts(1)
            final()

        @block.tensor
        def _(pe):
            def product(out, left, right, start=True, stop=True):
                pe.matmul(out, left(0), right(0), start=start, stop=False)
                pe.matmul(out, left(0), right(1), start=False, stop=False)
                return pe.matmul(out, left(1), right(0), start=False, stop=stop)

            pe.wait_ge(s_small, 16 * 8)
            pe.matmul(bank[:, 4, 0:D], wsmall[:, 0, :], wsmall[:, 1, :], start=True, stop=True).then_inc(s_prep_mm, 1)
            pe.wait_ge(s_const, 17)
            pe.transpose(bank[:, 5, 0:D], wsmall[:, 2, :], ident32[:]).then_inc(s_prep_mm, 1)
            for i in range(3):
                m = pe.transpose(bank[:, 6, i * D:i * D + D], wsmall[:, 3 + i, :], ident32[:])
            m.then_inc(s_prep_mm, 1)

            def norm_stage(l):
                S = L[l]

                def turn(u, p):
                    pe.wait_ge(S["lo"], u + 1)
                    past(pe, S["xts"], u - 1)
                    hl = unit(xn16, u)
                    for i in range(2):
                        dst = bank[:, 2 * p + i, :].bitcast(F16).rearrange("p (h k n) -> p h k n", h=2, k=K)
                        for h in range(2):
                            for k in range(K):
                                m = pe.transpose(dst[:, h, k, :], hl[:, i * K + k, h, :], ident16[:])
                    m.then_inc(S["xt"], 1)

                def logits(u, p):
                    pe.wait_ge(S["xts"], u + 1)
                    past(pe, S["lg"], u - 1)
                    for i in range(2):
                        x = xnt(l, 2 * u + i)
                        for k in range(K):
                            n = (i * K + k) * E
                            m = product(bank[:, 4 + p, n:n + E], lambda h: x[:, h, k * P:k * P + P],
                                        lambda h: rw16[:, l, h, :])
                    m.then_inc(S["logits"], 1)

                def body(u, j, p):
                    turn(u, p)
                    if within(u - 1, NU):
                        logits(u - 1, 1 - p)
                if l == 0:
                    pe.wait_ge(s_prep, 3)
                in_pairs(pe, NU, body)
                logits(NU - 1, 1)

            def ranks(l):
                pe.wait_ge(L[l]["routed"], 1)
                oh = onehot[:].rearrange("p t e -> p (t e)")
                pe.matmul(bank[:, 4, :], before16[:], oh, start=True, stop=True)
                pe.matmul(bank[:, 5, :], ones16[:, 0:P], oh, start=True, stop=True).then_inc(L[l]["rank"], 1)

            def attention():
                S = L[0]

                def t_of(b):
                    past(pe, S["v_lo"], b)
                    x = xnt(0, b)
                    product(bank[:, 7, :], lambda h: m16[:, h, :], lambda h: x[:, h, :]).then_inc(S["t_mm"], 1)

                def v_of(b):
                    pe.wait_ge(S["t_lo"], b + 1)
                    x = xnt(0, b)
                    for k in range(K):
                        m = product(bank[:, 7, k * D:k * D + D], lambda h: x[:, h, k * P:k * P + P],
                                    lambda h: wv16[:, h, :])
                    m.then_inc(S["v_mm"], 1)

                def scores(b, u, q, p):
                    pe.wait_ge(S["t_lo"], b + 1)
                    past(pe, S["expd"], u - 3)
                    x = xnt(0, b)
                    product(bank[:, q, :], lambda h: t16[:, p, h, q * P:q * P + P],
                            lambda h: x[:, h, :]).then_inc(S["score"], 1)

                def turn(u, q):
                    pe.wait_ge(S["expd"], u + 1)
                    past(pe, S["pt_lo"], u - 1)
                    for k in range(K):
                        m = pe.transpose(bank[:, 4 + q % 2, k * P:k * P + P], prob[:, q % 2, k * P:k * P + P],
                                         ident32[:])
                    m.then_inc(S["pt"], 1)

                def weigh(u, q, p):
                    pe.wait_ge(S["pt_lo"], u + 1)
                    past(pe, S["att"], u)
                    out = bank[:, 6, 0:D]
                    for k in range(K):
                        m = product(out, lambda h: pt16[:, q % 2, h, k, :], lambda h: v16[:, p, h, k, :],
                                    start=k == 0, stop=k == K - 1)
                    m.then_inc(S["pv"], 1)

                pe.wait_ge(s_prep, 6)
                pe.wait_ge(S["routed"], 3)
                t_of(0)
                v_of(0)
                scores(0, 0, 0, 0)
                scores(0, 1, 1, 0)

                def body(b, j, p):
                    for q in range(K):
                        u = K * b + q
                        if q == 0 and within(b + 1, NB):
                            t_of(b + 1)
                        if within(u + 2, NT):
                            if q < 2:
                                scores(b, u + 2, q + 2, p)
                            else:
                                scores(b + 1, u + 2, q - 2, 1 - p)
                        turn(u, q)
                        if q == 2 and within(b + 1, NB):
                            v_of(b + 1)
                        if within(u - 1, NT):
                            weigh(u - 1, (q + 3) % K, p if q else 1 - p)
                in_pairs(pe, NB, body)
                weigh(NT - 1, K - 1, 1)

            def linear_attention():
                S = LIN

                def qkv(b, i):
                    past(pe, S["qn"], 2 * b + i - 1)
                    x = xnt(1, b)
                    for k in range(KH * i, KH * i + KH):
                        m = product(bank[:, k, 0:3 * D], lambda h: x[:, h, k * P:k * P + P],
                                    lambda h: wqkv16[:, h, :])
                    m.then_inc(S["qkv"], 1)

                def state(b, p):
                    pe.wait_ge(S["sp"], 2 * b + 2)
                    past(pe, S["kvs"], b)
                    for k in range(K):
                        m = pe.matmul(bank[:, 4, 0:D + 2], sp[:, p, k, D:2 * D], v_one[:, p, k, :],
                                      start=k == 0, stop=k == K - 1)
                    m.then_inc(S["kv"], 1)
                    past(pe, S["qts"], b)
                    for k in range(K):
                        m = pe.transpose(bank[:, 5, k * P:k * P + P], sp[:, p, k, 0:D], ident32[:])
                    m.then_inc(S["qt"], 1)

                def read(b):
                    pe.wait_ge(S["kvs"], b + 1)
                    pe.wait_ge(S["qts"], b + 1)
                    past(pe, S["att"], b)
                    for k in range(K):
                        n = (k % 2) * (D + NH)
                        m = pe.matmul(bank[:, 6 + k // 2, n:n + D + NH], q_t[:, k * P:k * P + P], kvs[:],
                                      start=True, stop=True)
                    m.then_inc(S["out"], 1)

                def body(b, j, p):
                    for i in range(2):
                        if within(b, NB):
                            qkv(b, i)
                        if i == 0 and within(b - 2, NB):
                            read(b - 2)
                        if i == 1 and within(b - 1, NB):
                            state(b - 1, 1 - p)
                pe.wait_ge(L[1]["routed"], 3)
                in_pairs(pe, NB, body)
                body(NB, 0, 0)
                read(NB - 1)

            def experts(l):
                S = L[l]

                def turn(s, j, r):
                    pe.wait_ge(S[f"ld{r}"], 16 * (j + 1))
                    past(pe, S["xg_s"], s - 1)
                    dst = bank[:, r % 2, 0:TS].bitcast(F16).rearrange("p (h t n) -> p h t n", h=2, t=2)
                    for h in range(2):
                        for t in range(2):
                            m = pe.transpose(dst[:, h, t, :], xg[:, r % 2, t, h, :], ident16[:])
                    m.then_inc(S["xg_t"], 1)

                def experts_of(first, n):
                    src = (tile_expert[0:1, first:first + n] if isinstance(first, int)
                           else tile_expert[0:1, bass.ds(first, n)])
                    _, values = nc.values_load_multi_w_load_instructions(
                        src, engines=[pe.engine], min_val=0, max_val=E - 1,
                        skip_runtime_bounds_check_because="the routing clamps them to the number of experts")
                    return [bass.ds(value, 1) for value in values]

                def up(s, r, e):
                    pe.wait_ge(S["xg_s"], s + 1)
                    for g in range(2):
                        past(pe, S["h_lo"], 2 * s - 3 + g)
                        for c in range(2 * g, 2 * g + 2):
                            out = bank[:, 2 + 2 * (r % 2) + g, c % 2 * TS:c % 2 * TS + TS]
                            pe.matmul(out, bias16[:, e, c * P:c * P + P], ones16[:], start=True, stop=False)
                            m = product(out, lambda h: w1_16[:, e, h, c * P:c * P + P], lambda h: xgt[:, r % 2, h, :],
                                        start=False)
                        m.then_inc(S["up"], 1)

                def down(s, r, e):
                    pe.wait_ge(S["h_lo"], 2 * s + 2)
                    past(pe, S["y_v"], s - 1)
                    for t in range(2):
                        out = bank[:, 6 + r % 2, t * D:t * D + D]
                        pe.matmul(out, ones16[:, 0:P], bias16[:, e, FF:FF + D], start=True, stop=False)
                        for c in range(C):
                            m = product(out, lambda h: h16[:, r % 2, h, c, t * P:t * P + P],
                                        lambda h: w2_16[:, e, h, c, :], start=False, stop=c == C - 1)
                    m.then_inc(S["down"], 1)

                def step(s, j, r, e, at):
                    if within(s, MT):
                        turn(s, j, r)
                    if within(s - 1, MT):
                        up(s - 1, r + 1, e[at + 1])
                    if within(s - 2, MT):
                        down(s - 2, r, e[at])

                pe.wait_ge(S["routed"], 3)
                for part in ("w1_lo", "w2_lo", "b_lo"):
                    pe.wait_ge(S[part], E)
                if l == 0:
                    pe.wait_ge(S["att"], NT)
                else:
                    pe.wait_ge(LIN["att"], NB)
                e = experts_of(0, 3)
                for s in range(4):
                    step(s, 0, s, e, s - 2)
                with pe.Fori(1, MT // 4) as j:
                    e = experts_of(4 * j - 2, 5)
                    for r in range(4):
                        step(4 * j + r, j, r, e, r)
                last = MT // 4 * 4
                e = experts_of(last - 2, MT - last + 2)
                for s in range(last, MT + 2):
                    step(s, s // 4, s % 4, e, s - last)

            norm_stage(0)
            ranks(0)
            attention()
            experts(0)
            norm_stage(1)
            ranks(1)
            linear_attention()
            experts(1)


_INS = ['L0_attn_x', 'L0_attn_Wq', 'L0_attn_Wk', 'L0_attn_Wv', 'L0_ffn_gate_w', 'L0_ffn_gate_b', 'L0_ffn_w1',
        'L0_ffn_b1', 'L0_ffn_w2', 'L0_ffn_b2', 'L1_attn_W_qkv', 'L1_ffn_router_W', 'L1_ffn_router_b', 'L1_ffn_W1',
        'L1_ffn_b1', 'L1_ffn_W2', 'L1_ffn_b2']


def kernel(**inputs):
    import numpy as _np
    import concourse.bacc as _bacc
    from concourse import mybir as _mybir
    from concourse.bass_utils import run_bass_kernel_spmd as _run

    nc = _bacc.Bacc("TRN2", target_bir_lowering=False, num_devices=1)
    arrays, args = {}, []
    for name in _INS:
        a = _np.ascontiguousarray(inputs[name])
        arrays[f"in_{name}"] = a
        args.append(nc.dram_tensor(f"in_{name}", a.shape, _mybir.dt.from_np(a.dtype), kind="ExternalInput").ap())
    shape = inputs['L0_attn_x'].shape
    args.append(nc.dram_tensor("out", shape, _mybir.dt.float32, kind="ExternalOutput").ap())
    build(nc, *args)
    r = _run(nc, [arrays], core_ids=[0])
    return r.results[0]["out"]
```

```python
from contextlib import ExitStack

import concourse.bass as bass
from concourse import mybir

P = 128
ALU = mybir.AluOpType
ACT = mybir.ActivationFunctionType
AX = mybir.AxisListType
F32 = mybir.dt.float32
F16 = mybir.dt.float16
I32 = mybir.dt.int32
U32 = mybir.dt.uint32

RSQRT_SEED = 0x5F3759DF
NEWTON = 3


def past(engine, sem, value):
    if not (isinstance(value, int) and value <= 0):
        engine.wait_ge(sem, value)


def in_pairs(engine, n, body, peeled=1):
    for b in range(2 * peeled):
        body(b, b // 2, b % 2)
    with engine.Fori(peeled, n // 2 - 1) as j:
        for p in range(2):
            body(2 * j + p, j, p)
    for p in range(2):
        body(n - 2 + p, n // 2 - 1, p)


def within(b, n):
    return not isinstance(b, int) or 0 <= b < n


def build(nc, x_d, wq_d, wk_d, wv_d, gate_w, gate_b, ew1, eb1, ew2, eb2, wqkv_d, router_w, router_b,
          fw1, fb1, fw2, fb2, out_d):
    NB, TB, D = x_d.shape
    E, _, FF = ew1.shape
    NH = 16
    DH = D // NH
    K = TB // P
    NT = NB * K
    NU = NB // 2
    NJ = NU // 2
    KU = 2 * K
    KH = K // 2
    C = FF // P
    TS = 2 * P
    MT = NT * P // TS + E - 1
    SLOTS = MT * TS
    ROW = 2 * D + 2
    MTP = MT + 1
    LN_EPS, L2_EPS, K_EPS = 1e-5, 1e-12, 1e-6
    QK_SCALE = float(D) ** -0.5
    KV_SCALE = float(DH) ** -0.5
    assert D == P and K == 4 and NB % 4 == 0 and C == 4 and NU == E

    rows_d = [nc.dram_tensor(f"sorted_rows_{l}", (SLOTS, ROW), F16, kind="Internal").ap() for l in range(2)]
    y_d = [nc.dram_tensor(f"experts_y_{l}", (NT * P, D), F32, kind="Internal").ap() for l in range(2)]

    with ExitStack() as ctx:
        def sb(name, shape, dt):
            return ctx.enter_context(nc.sbuf_tensor(name, shape, dt))

        def sem(name):
            return ctx.enter_context(nc.semaphore(name))

        x_sb = sb("x_sb", [P, NT, D], F32)
        xn16 = sb("xn16", [P, NT, 2, D], F16)
        slots = sb("slots", [P, NB + 2, K * D], F32)
        w1_16 = sb("w1_16", [P, E, 2, FF], F16)
        w2_16 = sb("w2_16", [P, E, 2, C, D], F16)
        b1_rows = sb("b1_rows", [2 * E * C, P], F32)
        b1 = sb("b1", [P, 2, E, C], F32)
        b1_tile = sb("b1_tile", [P, 4, C], F32)
        b2 = sb("b2", [P, 2, E, D], F32)
        w_in = sb("w_in", [P, 2, 2, FF], F32)
        pool_carrier = sb("pool_carrier", [P, 3], F32)
        ident16 = sb("ident16", [P, P], F16)
        ident32 = sb("ident32", [P, P], F32)
        ones16 = sb("ones16", [P, P], F16)
        before16 = sb("before16", [P, P], F16)
        headmask = sb("headmask", [P, P], F32)
        headcol = sb("headcol", [P, NH], F32)
        from_last = sb("from_last", [P, E], F32)
        tile_no = sb("tile_no", [P, MTP], F32)
        xg = sb("xg", [P, 4, 2, ROW], F16)
        wsmall = xg[:, :, :, :].rearrange("p s t n -> p (s t n)").bitcast(F32)[:, 0:6 * D].rearrange(
            "p (i n) -> p i n", i=6)
        m16 = sb("m16", [P, 2, D], F16)
        wv16 = sb("wv16", [P, 2, D], F16)
        wqkv16 = sb("wqkv16", [P, 2, 3 * D], F16)
        rw32 = sb("rw32", [P, 2, E], F32)
        rw16 = sb("rw16", [P, 2, 2, E], F16)
        rbias = sb("rbias", [P, 2, E], F32)
        work = sb("work", [P, 2, KU * D], F32)
        silu = work[:, :, :].rearrange("p b (k d) -> p b k d", k=KU)
        stats = sb("stats", [P, 2, KU, 6], F32)
        mv = sb("mv", [P, 2, KU, 2], F32)
        nw_v = sb("nw_v", [P, 2 * KU], F32)
        nw_y = sb("nw_y", [P, 2 * KU], F32)
        nw_a = sb("nw_a", [P, 2 * KU], F32)
        shift = sb("shift", [P, 2 * KU], F32)
        lg = sb("lg", [P, NT, E], F32)
        best = sb("best", [P, NT], F32)
        expert = sb("expert", [P, NT], F32)
        second = sb("second", [P, NT // 2], F32)
        gate = sb("gate", [P, NT], F32)
        onehot = sb("onehot", [P, NT, E], F16)
        small = sb("small", [P, 8, E], F32)
        smalli = sb("smalli", [P, 2, E], I32)
        tile_expert = sb("tile_expert", [P, MTP], I32)
        pos = sb("pos", [P, NT], U32)
        pos_io = sb("pos_io", [P, 2, K], U32)
        row_io = w_in[:, :, :, :].rearrange("p a b n -> p a (b n)").bitcast(U32)[:, :, 0:K * ROW // 2].rearrange(
            "p a (k n) -> p a k n", k=K)
        token = sb("token", [P, NT], U32)
        ids = sb("ids", [P, 4, 2], U32)
        tv = sb("tv", [P, 4 * 2 * TB // 2], F32)
        t16 = tv[:, 0:2 * TB].bitcast(F16).rearrange("p (b h n) -> p b h n", b=2, h=2)
        xnf = tv[:, :].rearrange("p (b k d) -> p b k d", b=2, k=KU)
        v16 = tv[:, 2 * TB:4 * TB].bitcast(F16).rearrange("p (b h k n) -> p b h k n", b=2, h=2, k=K)
        prob = sb("prob", [P, 2, TB], F32)
        pt16 = sb("pt16", [P, 2, 2, K, P], F16)
        nmax = sb("nmax", [P, K], F32)
        rsum = sb("rsum", [P, K], F32)
        rden = sb("rden", [P, K], F32)
        qk_n = tv[:, :].rearrange("p (b k n) -> p b k n", b=2, k=K)
        sq = prob[:, :, :].rearrange("p a (k n) -> p a k n", k=KH)
        sp = work[:, :, :].rearrange("p b (k n) -> p b k n", k=K)
        v_one = sb("v_one", [P, 2, K, D + 2], F32)
        q_t = pt16[:, 0, :, :, :].rearrange("p b k n -> p (b k n)").bitcast(F32)
        kvs = sb("kvs", [P, D + NH], F32)
        ks = sb("ks", [P, 1], F32)
        ss = sb("ss", [P, 2, 3, KH * 2 * NH], F32)
        half30 = sb("half30", [P, 1], F32)
        rdn = sb("rdn", [P, K, NH], F32)
        xgt = sb("xgt", [P, 2, 2, TS], F16)
        h32 = pt16[:, :, :, :, :].rearrange("p a b k n -> p (a b k n)").bitcast(F32).rearrange(
            "p (a n) -> p a n", a=2)
        h16 = sb("h16", [P, 2, 2, C, TS], F16)
        y_sb = prob[:, :, 0:2 * D].rearrange("p s (t d) -> p s t d", t=2)
        y_back = h16[:, :, :, :, :].rearrange("p a b c n -> p (a b c n)").bitcast(F32).rearrange(
            "p (b k d) -> p b k d", b=2, k=KU)
        late = w1_16[:, :, :, :].rearrange("p e h n -> p (e h n)").bitcast(F32).rearrange(
            "p (b k d) -> p b k d", k=KU, d=D)
        y_last = [y_back[:, 0], y_back[:, 1], xnf[:, 0], xnf[:, 1]] + [late[:, i] for i in range(NU - 4)]
        LOADS = [(0,), (1, 2), (3, 4), tuple(range(5, NU))]
        GATED = (1, 3)

        scratch = [work[:, :, :].rearrange("p a n -> p (a n)"),
                   h16[:, :, :, :, :].rearrange("p a b c n -> p (a b c n)").bitcast(F32)]

        PER = SLOTS // P
        REPEAT = min(n for n in range(1, PER + 1) if PER % n == 0 and PER // n * ROW // 2 <= 2 * C * TS)
        pad_rows = h16[:, :, :, :, :].rearrange("p a b c n -> p (a b c n)").bitcast(I32)[
            :, 0:PER // REPEAT * ROW // 2].rearrange("p (r n) -> p r n", n=ROW // 2)

        bank = ctx.enter_context(nc.psum_tensor("bank", [P, 8, 512], F32))

        s_const = sem("s_const")
        s_carried = sem("s_carried")
        s_zeroed = [sem(f"s_zeroed{l}") for l in range(2)]
        s_small = sem("s_small")
        s_b2 = sem("s_b2")
        s_x = [sem(f"s_x{p}") for p in range(2)]
        s_prep = sem("s_prep")
        s_prep_mm = sem("s_prep_mm")
        s_step = sem("s_step")
        s_out = [sem(f"s_out{p}") for p in range(2)]
        NORM_STEPS = 2 * KU + 2 + 3 * NEWTON
        NAMES = ["w1_in0", "w2_in0", "w1_in1", "w2_in1", "w1_hi", "w2_hi", "w1_lo", "w2_lo",
                 "stats", "norm_step", "rstd", "xn", "hi", "lo", "xt", "xts", "logits", "lg", "onehot", "routed", "rank",
                 "staged", "scat00", "scat01", "scat02", "scat03", "scat10", "scat11", "scat12", "scat13",
                 "ld0", "ld1", "ld2", "ld3", "xg_t", "xg_s", "b1", "up", "h", "h_hi", "h_lo", "down", "y_v",
                 "ids", "st0", "st1", "st2", "st3"]
        ONLY = [["t_mm", "t_hi", "t_lo", "v_mm", "v_hi", "v_lo", "score", "rmax", "expd", "rcp", "pt", "pt_hi",
                 "pt_lo", "pv", "att"],
                ["y_in0", "y_in1", "silu", "times_att", "added0", "added1", "under_top", "gate_e"]]
        L = [{n: sem(f"{n}_{l}") for n in NAMES + ONLY[l]} for l in range(2)]
        LIN = {n: sem(f"lin_{n}") for n in ["qkv", "sq_v", "step", "rstep", "rdn", "r0", "qn", "exp", "sp", "kv", "qt", "kvs",
                                            "qts", "out", "att"]}
        FIN = {n: sem(f"fin_{n}") for n in ["y_in0", "y_in1", "y_in2", "y_in3", "gated", "silu", "times_att", "added0", "added1"]}

        def xnt(l, b):
            i = b + 2 - l
            v = slots[:, i:i + 1, :] if isinstance(i, int) else slots[:, bass.ds(i, 1), :]
            return v.bitcast(F16).rearrange("p o (h n) -> p (o h) n", h=2)

        def att(l, b):
            i = b + 1 - l
            v = slots[:, i:i + 1, :] if isinstance(i, int) else slots[:, bass.ds(i, 1), :]
            return v.rearrange("p o (k d) -> p (o k) d", k=K)

        def tiles(t, b):
            return t[:, bass.ds(K * b, K)] if not isinstance(b, int) else t[:, K * b:K * b + K]

        def unit(t, u):
            return t[:, bass.ds(KU * u, KU)] if not isinstance(u, int) else t[:, KU * u:KU * u + KU]

        def y_in(u):
            n = [u in units for units in LOADS].index(True)
            return FIN[f"y_in{n}"], 16 * len(LOADS[n])

        def unit_slots(first, u):
            i = 2 * u + first
            return slots[:, i:i + 2, :] if isinstance(i, int) else slots[:, bass.ds(i, 2), :]

        def unit_att(l, u):
            return unit_slots(1 - l, u).rearrange("p o (k d) -> p (o k) d", k=K)

        def unit_rows(t, u):
            src = t[bass.ds(2 * u, 2)] if not isinstance(u, int) else t[2 * u:2 * u + 2]
            return src.rearrange("o (k p) d -> p (o k) d", p=P)

        def weights_high(engine, copy, l, e, j, p):
            def of(t):
                return t[:, bass.ds(e, 1)] if not isinstance(e, int) else t[:, e:e + 1]
            S = L[l]
            engine.wait_ge(S[f"w1_in{p}"], 16 * (j + 1))
            copy(of(w1_16)[:, :, 0, :], w_in[:, p, 0:1, :]).then_inc(S["w1_hi"], 1)
            engine.wait_ge(S[f"w2_in{p}"], 16 * (j + 1))
            copy(of(w2_16).rearrange("p o h c d -> p o h (c d)")[:, :, 0, :], w_in[:, p, 1:2, :]).then_inc(S["w2_hi"], 1)

        def experts_of(engine, first, n):
            src = (tile_expert[0:1, first:first + n] if isinstance(first, int)
                   else tile_expert[0:1, bass.ds(first, n)])
            _, values = nc.values_load_multi_w_load_instructions(
                src, engines=[engine.engine], min_val=0, max_val=E - 1,
                skip_runtime_bounds_check_because="the routing clamps them to the number of experts")
            return [bass.ds(value, 1) for value in values]

        block = ctx.enter_context(nc.Block())

        @block.sync
        def _(sp_):
            def load_x(u, j, p):
                past(sp_, s_x[p], 16 * j)
                sp_.dma_start(unit(x_sb, u), unit_rows(x_d, u)).then_inc(s_x[p], 16)

            def load_expert(l, e, j, p, w1, w2):
                def of(t):
                    return t[bass.ds(e, 1)] if not isinstance(e, int) else t[e:e + 1]
                S = L[l]
                past(sp_, S["w1_lo"], e - 1)
                sp_.dma_start(w_in[:, p, 0, :], of(w1).rearrange("o d f -> d (o f)")).then_inc(S[f"w1_in{p}"], 16)
                past(sp_, S["w2_lo"], e - 1)
                sp_.dma_start(w_in[:, p, 1, :].rearrange("p (c d) -> p c d", c=C),
                              of(w2).rearrange("o (c p) d -> p (o c) d", p=P)).then_inc(S[f"w2_in{p}"], 16)

            def fill_rows(l):
                n = PER // REPEAT * ROW // 2
                sp_.dma_start(rows_d[l].bitcast(I32).rearrange("(p a r) d -> p a (r d)", p=P, a=1).rearrange(
                    "p a (c n) -> p (a c) n", n=n),
                    pad_rows.rearrange("p (o r) n -> p o (r n)", o=1).to_broadcast([P, REPEAT, n])
                    ).then_inc(s_zeroed[l], 16)

            for u in range(2):
                load_x(u, 0, u)
            for i, w in enumerate((wq_d, wk_d, wv_d)):
                sp_.dma_start(wsmall[:, i, :], w).then_inc(s_small, 16)
            sp_.dma_start(wsmall[:, 3:6, :], wqkv_d.rearrange("(g o) d -> o g d", g=3)).then_inc(s_small, 16)
            for l, (w, b) in enumerate(((gate_w, gate_b), (router_w, router_b))):
                sp_.dma_start(rw32[:, l, :], w).then_inc(s_small, 16)
                sp_.dma_start(rbias[:, l, :], b.rearrange("(o e) -> o e", o=1).to_broadcast([P, E])).then_inc(s_small, 16)
            for l, b in enumerate((eb1, fb1)):
                sp_.dma_start(b1_rows[l * E * C:(l + 1) * E * C, :], b.rearrange("e (c p) -> (e c) p", p=P)).then_inc(
                    s_small, 16)
            weights = (ew1, ew2)
            for u in range(2):
                load_x(2 + u, 1, u)
            for e in range(2):
                load_expert(0, e, 0, e, *weights)
            with sp_.Fori(1, NJ - 1) as j:
                for p in range(2):
                    load_x(2 * j + 2 + p, j + 1, p)
                for p in range(2):
                    load_expert(0, 2 * j + p, j, p, *weights)
            for p in range(2):
                load_expert(0, E - 2 + p, NJ - 1, p, *weights)
            sp_.wait_ge(s_const, 2)
            fill_rows(0)
            fill_rows(1)
            for l, b in enumerate((eb2, fb2)):
                sp_.dma_start(b2[:, l, :, :].rearrange("p e d -> p (e d)"),
                              b.rearrange("(o e) d -> o (e d)", o=1).to_broadcast([P, E * D])).then_inc(s_b2, 16)

            def experts(l):
                def rows(t, s):
                    part = t[bass.ds(s * TS, TS)] if not isinstance(s, int) else t[s * TS:s * TS + TS]
                    return part.rearrange("(t p) n -> p t n", p=P)

                def step(s, j, r):
                    past(sp_, L[l]["xg_t"], s - 3)
                    past(sp_, L[l]["ids"], s - 3)
                    src = rows_d[l][bass.ds(s * TS, TS)] if not isinstance(s, int) else rows_d[l][s * TS:s * TS + TS]
                    sp_.dma_start(xg[:, r, :, :], src.rearrange("(t p) n -> p t n", p=P)).then_inc(
                        L[l][f"ld{r}"], 16)
                for p in range(2):
                    for k in range(K):
                        sp_.wait_ge(L[l][f"scat{p}{k}"], 16 * NB // 2)
                for s in range(4):
                    step(s, 0, s)
                with sp_.Fori(1, MT // 4) as j:
                    for r in range(4):
                        step(4 * j + r, j, r)
                for s in range(MT // 4 * 4, MT):
                    step(s, s // 4, s % 4)
                for r in range(4):
                    sp_.wait_ge(L[l][f"st{r}"], 32 * len(range(r, MT, 4)))

            def load_y(l, u, slot, loaded):
                src = y_d[l][bass.ds(u * KU * P, KU * P)] if not isinstance(u, int) else \
                    y_d[l][u * KU * P:(u + 1) * KU * P]
                sp_.dma_start(slot, src.rearrange("(k p) d -> p k d", p=P)).then_inc(loaded, 16)

            def load_pair(j):
                for p in range(2):
                    past(sp_, L[1]["silu"], 2 * j + p - 1)
                    load_y(0, 2 * j + p, y_back[:, p, :, :], L[1][f"y_in{p}"])

            experts(0)
            weights = (fw1, fw2)
            for j in range(2):
                load_pair(j)
            for e in range(2):
                load_expert(1, e, 0, e, *weights)
            with sp_.Fori(1, NJ - 1) as j:
                load_pair(j + 1)
                for p in range(2):
                    load_expert(1, 2 * j + p, j, p, *weights)
            for p in range(2):
                load_expert(1, E - 2 + p, NJ - 1, p, *weights)
            experts(1)

            def store(u):
                sp_.wait_ge(FIN[f"added{u % 2}"], u // 2 + 1)
                sp_.dma_start(unit_rows(out_d, u), unit(x_sb, u)).then_inc(s_out[u % 2], 16)

            for u in range(NU):
                load_y(1, u, y_last[u], y_in(u)[0])
            for u in range(NU):
                store(u)
            for p in range(2):
                sp_.wait_ge(s_out[p], 16 * NU // 2)

        @block.gpsimd
        def _(pool):
            g = nc.gpsimd
            g.memset(pool_carrier[:], 0.0)
            g.memset(pad_rows, 0).then_inc(s_const, 1)
            pool.wait_ge(s_const, 1)
            g.memset(pad_rows[:, :, D:D + 1], NT * P).then_inc(s_const, 1)
            g.memset(ones16[:], 1.0).then_inc(s_const, 1)
            g.memset(ident32[:], 0.0).then_inc(s_const, 1)
            g.memset(headmask[:], KV_SCALE).then_inc(s_const, 1)
            g.memset(headcol[:], 1.0).then_inc(s_const, 1)
            g.memset(v_one[:], 1.0).then_inc(s_const, 1)
            g.iota(from_last[:], [[-1, E]], base=E, channel_multiplier=0,
                   allow_small_or_imprecise_dtypes=True).then_inc(s_const, 1)
            g.iota(tile_no[:], [[1, MTP]], base=0, channel_multiplier=0,
                   allow_small_or_imprecise_dtypes=True).then_inc(s_const, 1)
            g.iota(token[:].bitcast(I32), [[P, NT]], base=0, channel_multiplier=1).then_inc(s_const, 1)
            pool.wait_ge(s_const, 10)
            g.affine_select(out=ident32[:], in_=ident32[:], compare_op=ALU.not_equal, fill=1.0, base=0,
                            pattern=[[-1, P]], channel_multiplier=1).then_inc(s_const, 1)
            g.affine_select(out=before16[:], in_=ones16[:], compare_op=ALU.is_gt, fill=0.0, base=0,
                            pattern=[[1, P]], channel_multiplier=-1).then_inc(s_const, 1)
            hm = headmask[:, :].rearrange("p (h d) -> p h d", h=NH)
            g.affine_select(out=hm, in_=hm, compare_op=ALU.is_ge, fill=0.0, base=0,
                            pattern=[[-DH, NH], [0, DH]], channel_multiplier=1).then_inc(s_const, 1)
            g.affine_select(out=headcol[:], in_=headcol[:], compare_op=ALU.is_ge, fill=0.0, base=0,
                            pattern=[[-DH, NH]], channel_multiplier=1).then_inc(s_const, 1)
            pool.wait_ge(s_const, 14)
            g.affine_select(out=hm, in_=hm, compare_op=ALU.is_ge, fill=0.0, base=DH - 1,
                            pattern=[[DH, NH], [0, DH]], channel_multiplier=-1).then_inc(s_const, 1)
            g.affine_select(out=headcol[:], in_=headcol[:], compare_op=ALU.is_ge, fill=0.0, base=DH - 1,
                            pattern=[[DH, NH]], channel_multiplier=-1).then_inc(s_const, 1)
            g.tensor_copy(ident16[:], ident32[:]).then_inc(s_const, 1)

            def carry(i):
                return g.tensor_tensor(pool_carrier[:, i:i + 1], pool_carrier[:, 0:1], pool_carrier[:, 0:1], ALU.add)

            def weights_low(l, e, p):
                def of(t):
                    return t[:, bass.ds(e, 1)] if not isinstance(e, int) else t[:, e:e + 1]
                S = L[l]
                w1o = of(w1_16)
                w2o = of(w2_16).rearrange("p o h c d -> p o h (c d)")
                pool.wait_ge(S["w1_hi"], e + 1)
                g.tensor_tensor(w1o[:, :, 1, :], w_in[:, p, 0:1, :], w1o[:, :, 0, :], ALU.subtract).then_inc(
                    S["w1_lo"], 1)
                pool.wait_ge(S["w2_hi"], e + 1)
                g.tensor_tensor(w2o[:, :, 1, :], w_in[:, p, 1:2, :], w2o[:, :, 0, :], ALU.subtract).then_inc(
                    S["w2_lo"], 1)

            def add_up(S, u, t):
                pool.wait_ge(S["times_att"], u + 1)
                x = unit(x_sb, u)
                g.tensor_tensor(x, x, t, ALU.add).then_inc(S["added0"], 1)

            def norm_stage(l):
                S = L[l]

                def body(j):
                    if within(j - 1, NJ):
                        weights_low(l, 2 * j - 1, 1)
                    if l == 1 and within(j + 1, NJ):
                        add_up(S, 2 * j + 2, silu[:, 0, :, :])
                    for p in range(2):
                        u = 2 * j + p
                        pool.wait_ge(S["hi"], u + 1)
                        hl = unit(xn16, u)
                        g.tensor_tensor(hl[:, :, 1, :], xnf[:, p, :, :], hl[:, :, 0, :], ALU.subtract).then_inc(
                            S["lo"], 1)
                    weights_low(l, 2 * j, 0)
                if l == 1:
                    add_up(S, 0, silu[:, 0, :, :])
                for j in range(NJ):
                    body(j)
                weights_low(l, E - 1, 1)

            def scatter(l):
                pool.wait_ge(L[l]["routed"], 3)
                pool.wait_ge(s_zeroed[l], 16)
                for part in ("w1_lo", "w2_lo"):
                    pool.wait_ge(L[l][part], E)

                def body(b, j, p):
                    for k in range(K):
                        past(pool, L[l][f"scat{p}{k}"], 16 * j)
                    st = L[l]["staged"]
                    g.tensor_copy(pos_io[:, p, :], tiles(pos, b)).then_inc(st, 1)
                    g.tensor_copy(row_io[:, p, :, 0:D], tiles(xn16, b).rearrange("p k h d -> p k (h d)").bitcast(U32)
                                  ).then_inc(st, 1)
                    g.tensor_copy(row_io[:, p, :, D:D + 1], tiles(token, b).unsqueeze(2)).then_inc(st, 1)
                    pool.wait_ge(st, 3 * b + 3)
                    carry(1)
                    for k in range(K):
                        g.indirect_dma_start(rows_d[l][:, :], bass.IndirectOffsetOnAxis(pos_io[:, p, k:k + 1], 0),
                                             row_io[:, p, k, :].bitcast(F16), None).then_inc(L[l][f"scat{p}{k}"], 16)
                in_pairs(pool, NB, body)

            def experts(l):
                S = L[l]

                def bias(r, e):
                    g.tensor_copy(b1_tile[:, r, :].unsqueeze(1), b1[:, l, e, :]).then_inc(S["b1"], 1)

                def step(s, r, e):
                    pool.wait_ge(S["y_v"], s + 1)
                    past(pool, s_carried, MT * l + s)
                    carry(2).then_inc(s_carried, 1)
                    for t in range(2):
                        g.indirect_dma_start(y_d[l][:, :], bass.IndirectOffsetOnAxis(ids[:, r, t:t + 1], 0),
                                             y_sb[:, r % 2, t, :], None, bounds_check=NT * P - 1,
                                             oob_is_err=False).then_inc(S[f"st{r}"], 16)
                    if within(s + 3, MT):
                        bias((r + 3) % 4, e)
                pool.wait_ge(S["routed"], 4)
                pool.wait_ge(s_prep, 7)
                e = experts_of(pool, 0, 7)
                for r in range(3):
                    bias(r, e[r])
                for s in range(4):
                    step(s, s, e[s + 3])
                with pool.Fori(1, MT // 4) as j:
                    e = experts_of(pool, 4 * j + 3, 4)
                    for r in range(4):
                        step(4 * j + r, r, e[r])
                assert MT % 4 == 3
                for s in range(MT // 4 * 4, MT):
                    step(s, s % 4, None)

            for l in range(2):
                norm_stage(l)
                scatter(l)
                experts(l)
            for u in range(0, NU, 2):
                add_up(FIN, u, y_last[u])

        @block.scalar
        def _(act):
            a = nc.scalar

            def norm_stage(l):
                S = L[l]

                def silu_of(u, j, p):
                    act.wait_ge(S[f"y_in{p}"], 16 * (j + 1))
                    past(act, S[f"added{p}"], j)
                    a.activation(silu[:, p, :, :], y_back[:, p, :, :], ACT.Silu,
                                 scale=2.0).then_inc(S["silu"], 1)

                def normalised(u, j, p):
                    act.wait_ge(S["rstd"], j + 1)
                    past(act, S["lo"], u - 1)
                    x = unit(x_sb, u)
                    for k in range(KU):
                        n = p * KU + k
                        a.activation(xnf[:, p, k, :], x[:, k, :], ACT.Identity, scale=nw_y[:, n:n + 1],
                                     bias=shift[:, n:n + 1]).then_inc(S["xn"], 1)

                def to_sbuf(u, p):
                    act.wait_ge(S["xt"], u + 1)
                    a.activation(unit_slots(2 - l, u).bitcast(F16), bank[:, 2 * p:2 * p + 2, :].bitcast(F16),
                                 ACT.Copy).then_inc(S["xts"], 1)

                def body(j):
                    if l == 1 and within(j + 1, NJ):
                        for p in range(2):
                            silu_of(2 * j + 2 + p, j + 1, p)
                    for p in range(2):
                        if 2 * j + p < NU - 1:
                            normalised(2 * j + p, j, p)
                    if within(j - 1, NJ):
                        for p in range(2):
                            to_sbuf(2 * j - 2 + p, p)
                    if l == 1 and j < NJ - 1:
                        experts_high(j)

                def experts_high(j):
                    for p in range(2):
                        weights_high(act, lambda out, in_: a.activation(out, in_, ACT.Copy), l, 2 * j + p, j, p)

                if l == 1:
                    for p in range(2):
                        silu_of(p, 0, p)
                for j in range(NJ):
                    body(j)
                for p in range(2):
                    to_sbuf(NU - 2 + p, p)
                if l == 1:
                    experts_high(NJ - 1)
                    nc.scalar.preload_act_table_set("natural_log_exp_and_others")
                if l == 1:
                    act.wait_ge(S["under_top"], 2)
                    a.activation(lg[:], lg[:], ACT.Exp).then_inc(S["gate_e"], 1)

            def attention():
                S = L[0]

                def t_high(b, p):
                    act.wait_ge(S["t_mm"], b + 1)
                    a.activation(t16[:, p, 0, :], bank[:, 7, :], ACT.Copy).then_inc(S["t_hi"], 1)

                def v_high(b, p):
                    act.wait_ge(S["v_mm"], b + 1)
                    a.activation(v16[:, p, 0, :, :], bank[:, 7, :].rearrange("p (k d) -> p k d", k=K),
                                 ACT.Copy).then_inc(S["v_hi"], 1)

                def softmax_exp(u, q):
                    act.wait_ge(S["rmax"], u + 1)
                    past(act, S["pt"], u - 1)
                    a.activation(prob[:, q % 2, :], bank[:, q, :], ACT.Exp, bias=nmax[:, q:q + 1],
                                 accum_out=rsum[:, q:q + 1]).then_inc(S["expd"], 1)

                def result(b, u, q):
                    act.wait_ge(S["rcp"], u + 1)
                    act.wait_ge(S["pv"], u + 1)
                    a.activation(att(0, b)[:, q, :], bank[:, 6, 0:D], ACT.Copy,
                                 scale=rden[:, q:q + 1]).then_inc(S["att"], 1)

                t_high(0, 0)
                v_high(0, 0)
                softmax_exp(0, 0)

                def body(b, j, p):
                    for q in range(K):
                        u = K * b + q
                        if within(u - 2, NT):
                            result(b if q >= 2 else b - 1, u - 2, (q + 2) % K)
                        if within(u + 1, NT):
                            softmax_exp(u + 1, (q + 1) % K)
                        if q == 0 and within(b + 1, NB):
                            t_high(b + 1, 1 - p)
                        act.wait_ge(S["pt"], u + 1)
                        past(act, S["pv"], u - 1)
                        a.activation(pt16[:, q % 2, 0, :, :],
                                     bank[:, 4 + q % 2, :].rearrange("p (k n) -> p k n", k=K),
                                     ACT.Copy).then_inc(S["pt_hi"], 1)
                        if q == 2 and within(b + 1, NB):
                            v_high(b + 1, 1 - p)
                in_pairs(act, NB, body)
                result(NB - 1, NT - 2, 2)
                result(NB - 1, NT - 1, 3)

            def linear_attention():
                S = LIN

                def front(b, i, p):
                    h = 2 * b + i
                    act.wait_ge(S["qkv"], h + 1)
                    qkv = bank[:, KH * i:KH * i + KH, :]
                    past(act, S["step"], 4 * (h - 2) + 1)
                    a.activation(sq[:, i, :, :], qkv[:, :, 0:2 * D], ACT.Square).then_inc(S["sq_v"], 1)
                    past(act, S["kv"], b - 1)
                    a.activation(v_one[:, p, KH * i:KH * i + KH, 0:D], qkv[:, :, 2 * D:3 * D],
                                 ACT.Copy).then_inc(S["sq_v"], 1)

                def inv_norm(b, i):
                    h = 2 * b + i
                    r = ss[:, i, 1, :]
                    act.wait_ge(S["step"], 4 * h + 2)
                    a.activation(r, ss[:, i, 0, :], ACT.Ln, scale=2.0 ** 30).then_inc(S["r0"], 1)
                    act.wait_ge(S["r0"], 3 * h + 1)
                    a.activation(r, r, ACT.Exp, scale=-0.5, bias=half30[:, 0:1]).then_inc(S["r0"], 1)
                    act.wait_ge(S["r0"], 3 * h + 2)
                    a.activation(ss[:, i, 2, :], r, ACT.Square).then_inc(S["r0"], 1)

                def softplus(b, i, p):
                    h = 2 * b + i
                    act.wait_ge(S["qn"], h + 1)
                    x = qk_n[:, p, KH * i:KH * i + KH, :]
                    a.activation(x, x, ACT.Exp).then_inc(S["exp"], 1)
                    act.wait_ge(S["exp"], h + 1)
                    a.activation(sp[:, p, KH * i:KH * i + KH, :], x, ACT.Ln, bias=1.0).then_inc(S["sp"], 1)

                def q_out(b):
                    act.wait_ge(S["qt"], b + 1)
                    past(act, S["out"], b)
                    a.activation(q_t[:, :], bank[:, 5, :], ACT.Copy).then_inc(S["qts"], 1)

                def body(b, j, p):
                    for i in range(2):
                        if within(b, NB):
                            inv_norm(b, i)
                        if i == 0 and within(b, NB):
                            front(b, 1, p)
                        if i == 1 and within(b + 1, NB):
                            front(b + 1, 0, 1 - p)
                        if i == 0 and within(b - 1, NB):
                            softplus(b - 1, 1, 1 - p)
                        if i == 1 and within(b, NB):
                            softplus(b, 0, p)
                        if i == 1 and within(b - 1, NB):
                            q_out(b - 1)
                front(0, 0, 0)
                in_pairs(act, NB, body)
                body(NB, 0, 0)

            def experts(l):
                S = L[l]

                def step(u, r):
                    act.wait_ge(S["b1"], u + 1)
                    for g in range(2):
                        act.wait_ge(S["up"], 2 * u + g + 1)
                        past(act, S["h_lo"], 2 * u - 1 + g)
                        for c in range(2):
                            a.activation(h32[:, g, c * TS:c * TS + TS],
                                         bank[:, 2 + 2 * (r % 2) + g, c * TS:c * TS + TS],
                                         ACT.Gelu if l == 0 else ACT.Relu,
                                         bias=b1_tile[:, r, 2 * g + c:2 * g + c + 1]).then_inc(S["h"], 1)
                nc.scalar.preload_act_table_set("gelu_and_others" if l == 0 else "silu_and_others")
                for u in range(4):
                    step(u, u)
                with act.Fori(1, MT // 4) as j:
                    for r in range(4):
                        step(4 * j + r, r)
                for u in range(MT // 4 * 4, MT):
                    step(u, u % 4)

            def final():
                for u in range(NU):
                    y = y_last[u]
                    if u in GATED:
                        act.wait_ge(FIN["gated"], GATED.index(u) + 1)
                        a.activation(y, y, ACT.Silu).then_inc(FIN["silu"], 1)
                        continue
                    act.wait_ge(*y_in(u))
                    gates = unit(gate, u)
                    for k in range(KU):
                        last = a.activation(y[:, k, :], y[:, k, :], ACT.Silu, scale=gates[:, k:k + 1])
                    last.then_inc(FIN["silu"], 1)

            norm_stage(0)
            attention()
            experts(0)
            norm_stage(1)
            linear_attention()
            experts(1)
            final()

        @block.vector
        def _(dve):
            v = nc.vector
            count = [0]

            def link(ins):
                count[0] += 1
                ins.then_inc(s_step, 1)
                dve.wait_ge(s_step, count[0])

            def pair(dst, src):
                link(v.tensor_copy(dst[:, 0], src))
                v.tensor_tensor(dst[:, 1], src, dst[:, 0], ALU.subtract).then_inc(s_prep, 1)

            def small_weights():
                v.memset(half30[:], 15.0 * 0.6931471805599453).then_inc(s_prep, 1)
                dve.wait_ge(s_small, 16 * 10)
                for l in range(2):
                    pair(rw16[:, l], rw32[:, l, :])
                dve.wait_ge(s_prep_mm, 1)
                link(v.tensor_scalar(wsmall[:, 0, :], bank[:, 4, 0:D], QK_SCALE, None, ALU.mult))
                pair(m16, wsmall[:, 0, :])
                dve.wait_ge(s_prep_mm, 2)
                pair(wv16, bank[:, 5, 0:D])
                dve.wait_ge(s_prep_mm, 3)
                pair(wqkv16, bank[:, 6, 0:3 * D])
                dve.wait_ge(s_prep_mm, 4)
                v.tensor_copy(b1[:, :, :, :].rearrange("p l e c -> p (l e c)"), bank[:, 7, 0:2 * E * C]).then_inc(s_prep, 1)

            def weigh(S, t, u, p, l):
                dve.wait_ge(S["silu"], u + 1)
                v.tensor_tensor(t, t, unit_att(l, u), ALU.mult).then_inc(S["times_att"], 1)
                if p == 1:
                    dve.wait_ge(S["times_att"], u + 1)
                    x = unit(x_sb, u)
                    v.tensor_tensor(x, x, t, ALU.add).then_inc(S["added1"], 1)

            def norm_stage(l):
                S = L[l]

                def statistics(j):
                    for p in range(2):
                        u = 2 * j + p
                        if l == 0:
                            dve.wait_ge(s_x[p], 16 * (j + 1))
                        else:
                            dve.wait_ge(S[f"added{p}"], j + 1)
                        x = unit(x_sb, u)
                        for k in range(KU):
                            v.bn_stats(stats[:, p, k, :], x[:, k, :]).then_inc(S["stats"], 1)

                def normalised(u):
                    dve.wait_ge(S["rstd"], NJ)
                    dve.wait_ge(S["lo"], u - 1)
                    for k in range(KU):
                        n = KU + k
                        ins = v.tensor_scalar(xnf[:, 1, k, :], unit(x_sb, u)[:, k, :], nw_y[:, n:n + 1],
                                              shift[:, n:n + 1], ALU.mult, ALU.add)
                    link(ins)

                def high(u, p):
                    if u < NU - 1:
                        dve.wait_ge(S["xn"], KU * (u + 1))
                    v.tensor_copy(unit(xn16, u)[:, :, 0, :], xnf[:, p, :, :]).then_inc(S["hi"], 1)

                def body(j):
                    n = [0]

                    def step(ins, wait=True):
                        n[0] += 1
                        ins.then_inc(S["norm_step"], 1)
                        if wait:
                            dve.wait_ge(S["norm_step"], NORM_STEPS * j + n[0])

                    dve.wait_ge(S["stats"], 2 * KU * (j + 1))
                    for p in range(2):
                        for k in range(KU):
                            step(v.bn_aggr(mv[:, p, k, :], stats[:, p, k, :]), wait=p and k == KU - 1)
                    m = mv[:, :, :, :].rearrange("p a k t -> p (a k) t")
                    vv, y, w = nw_v[:], nw_y[:], nw_a[:]
                    past(dve, S["xn"], 2 * KU * j)
                    step(v.tensor_scalar(vv, m[:, :, 1], LN_EPS, None, ALU.add))
                    step(v.tensor_scalar(y.bitcast(I32), vv.bitcast(I32), -0.5, float(RSQRT_SEED), ALU.mult, ALU.add))
                    for _ in range(NEWTON):
                        step(v.tensor_tensor(w, y, y, ALU.mult))
                        step(v.scalar_tensor_tensor(out=w, in0=w, scalar=-0.5, in1=vv, op0=ALU.mult, op1=ALU.mult))
                        step(v.scalar_tensor_tensor(out=y, in0=w, scalar=1.5, in1=y, op0=ALU.add, op1=ALU.mult))
                    v.scalar_tensor_tensor(out=shift[:], in0=m[:, :, 0], scalar=-1.0, in1=y,
                                           op0=ALU.mult, op1=ALU.mult).then_inc(S["rstd"], 1)
                    assert n[0] == NORM_STEPS
                    if l == 0 and j == 0:
                        small_weights()
                    if l == 1 and within(j + 1, NJ):
                        for p in range(2):
                            weigh(S, silu[:, p, :, :], 2 * j + 2 + p, p, 0)
                    if within(j - 2, NJ):
                        for p in range(2):
                            keep_logits(2 * j - 4 + p, p)
                    if l == 0 and within(j + 1, NJ):
                        statistics(j + 1)
                    if j == NJ - 1:
                        normalised(NU - 1)
                    high(2 * j, 0)
                    if l == 0:
                        weights_high(dve, v.tensor_copy, l, 2 * j, j, 0)
                    elif within(j + 1, NJ):
                        statistics(j + 1)
                    high(2 * j + 1, 1)
                    if l == 0:
                        weights_high(dve, v.tensor_copy, l, 2 * j + 1, j, 1)

                def keep_logits(u, p):
                    dve.wait_ge(S["logits"], u + 1)
                    v.tensor_tensor(unit(lg, u), bank[:, 4 + p, 0:KU * E].rearrange("p (k e) -> p k e", k=KU),
                                    rbias[:, l, :].unsqueeze(1).to_broadcast([P, KU, E]), ALU.add).then_inc(S["lg"], 1)

                if l == 1:
                    for p in range(2):
                        weigh(S, silu[:, p, :, :], p, p, 0)
                statistics(0)
                for j in range(NJ):
                    body(j)
                choose(l, 0)
                for u in range(NU - 4, NU):
                    keep_logits(u, u % 2)

            def choose(l, half):
                S = L[l]
                dve.wait_ge(S["lg"], NU // 2 * (half + 1))
                of = slice(half * NT // 2, (half + 1) * NT // 2)
                wide = [P, NT // 2, E]
                values, one = lg[:, of, :], onehot[:, of, :]
                top_value, chosen = best[:, of], expert[:, of]
                mask = scratch[l][:, 0:NT // 2 * E].rearrange("p (t e) -> p t e", e=E)
                from_last_of_all = from_last[:].unsqueeze(1).to_broadcast(wide)

                def spread(t):
                    return t.unsqueeze(2).to_broadcast(wide)

                def top(out):
                    link(v.tensor_reduce(top_value, values, AX.X, ALU.max))
                    link(v.tensor_tensor(mask, values, spread(top_value), ALU.is_equal))
                    link(v.tensor_tensor(mask, mask, from_last_of_all, ALU.mult))
                    link(v.tensor_reduce(out, mask, AX.X, ALU.max))

                top(chosen)
                if l == 0:
                    link(v.tensor_tensor(mask, from_last_of_all, spread(chosen), ALU.is_equal))
                    link(v.scalar_tensor_tensor(out=values, in0=mask, scalar=-3.0e38, in1=values, op0=ALU.mult,
                                                op1=ALU.add))
                    top(second[:])
                    link(v.tensor_tensor(chosen, chosen, second[:], ALU.min))
                if l == 1:
                    v.tensor_tensor(values, values, spread(top_value), ALU.subtract).then_inc(S["under_top"], 1)
                v.tensor_tensor(one, spread(chosen), from_last_of_all, ALU.is_equal).then_inc(S["onehot"], 1)

            def routing(l):
                S = L[l]
                tot, incl, rank = (scratch[l][:, n * NT * E:(n + 1) * NT * E] for n in range(3))
                cmp = scratch[l][:, 3 * NT * E:3 * NT * E + MTP * E].rearrange("p (t e) -> p t e", e=E)
                inc_v = incl.rearrange("p (e t) -> p e t", e=E)
                start, n, nt, tc, delta = (small[:, i, :] for i in range(5))

                def counts():
                    dve.wait_ge(S["rank"], 1)
                    v.tensor_copy(tot.rearrange("p (e t) -> p t e", e=E),
                                  bank[:, 5, :].rearrange("p (t e) -> p t e", e=E)).then_inc(S["routed"], 1)
                    v.tensor_copy(rank, bank[:, 6, :]).then_inc(S["routed"], 1)

                def expert_starts():
                    dve.wait_ge(S["routed"], 2)
                    link(v.tensor_tensor_scan(incl, tot, tot, 0.0, ALU.add, ALU.max))
                    ends = inc_v[:, :, NT - 1]
                    link(v.memset(start, 0.0))
                    link(v.tensor_copy(start[:, 1:E], ends[:, 0:E - 1]))
                    link(v.tensor_tensor(n, ends, start, ALU.subtract))
                    link(v.tensor_scalar(smalli[:, 0, :], n, float(TS - 1), None, ALU.add))
                    link(v.tensor_scalar(smalli[:, 1, :], smalli[:, 0, :], TS.bit_length() - 1, None,
                                         ALU.arith_shift_right))

                def expert_tiles():
                    link(v.tensor_copy(nt, smalli[:, 1, :]))
                    link(v.tensor_tensor_scan(tc, nt, nt, 0.0, ALU.add, ALU.max))
                    link(v.tensor_tensor(delta, tc, nt, ALU.subtract))
                    link(v.scalar_tensor_tensor(out=delta, in0=delta, scalar=float(TS), in1=start, op0=ALU.mult,
                                                op1=ALU.subtract))
                    link(v.tensor_tensor(incl, incl, tot, ALU.subtract))

                def token_slots():
                    link(v.tensor_tensor(inc_v, inc_v, delta.unsqueeze(2).to_broadcast([P, E, NT]), ALU.add))
                    te = incl.rearrange("p (e t) -> p t e", e=E)
                    tt = tot.rearrange("p (t e) -> p t e", e=E)
                    link(v.tensor_tensor(tt, te, rank.rearrange("p (t e) -> p t e", e=E), ALU.add))
                    link(v.tensor_tensor(tt, tt, onehot[:], ALU.mult))
                    with nc.allow_low_precision(reason="whole numbers below 2^24, summed in float32"):
                        v.tensor_reduce(pos[:], tt, AX.X, ALU.add).then_inc(S["routed"], 1)

                def tile_experts():
                    link(v.tensor_tensor(cmp, tile_no[:].unsqueeze(2).to_broadcast([P, MTP, E]),
                                         tc.unsqueeze(1).to_broadcast([P, MTP, E]), ALU.is_ge))
                    link(v.tensor_reduce(rank[:, 0:MTP], cmp, AX.X, ALU.add))
                    v.tensor_scalar(tile_expert[:], rank[:, 0:MTP], float(E - 1), None, ALU.min).then_inc(
                        S["routed"], 1)
                    if l == 1:
                        dve.wait_ge(S["gate_e"], 1)
                        link(v.tensor_reduce(gate[:], lg[:], AX.X, ALU.add))
                        link(v.reciprocal(gate[:], gate[:]))
                return counts, expert_starts, expert_tiles, token_slots, tile_experts

            def attention():
                S = L[0]

                def t_low(b, p):
                    dve.wait_ge(S["t_hi"], b + 1)
                    v.tensor_tensor(t16[:, p, 1, :], bank[:, 7, :], t16[:, p, 0, :], ALU.subtract).then_inc(S["t_lo"], 1)

                def v_low(b, p):
                    dve.wait_ge(S["v_hi"], b + 1)
                    v.tensor_tensor(v16[:, p, 1, :, :], bank[:, 7, :].rearrange("p (k d) -> p k d", k=K),
                                    v16[:, p, 0, :, :], ALU.subtract).then_inc(S["v_lo"], 1)

                def row_max(u, q):
                    dve.wait_ge(S["score"], u + 1)
                    past(dve, S["expd"], u - 3)
                    v.tensor_reduce(nmax[:, q:q + 1], bank[:, q, :], AX.X, ALU.max, negate=True).then_inc(S["rmax"], 1)

                counts, *stages = routing(0)
                t_low(0, 0)
                choose(0, 1)
                v_low(0, 0)
                counts()
                row_max(0, 0)
                row_max(1, 1)

                def body(b, j, p):
                    for q in range(K):
                        u = K * b + q
                        if within(u + 2, NT):
                            row_max(u + 2, (q + 2) % K)
                        if q == 0 and within(b + 1, NB):
                            t_low(b + 1, 1 - p)
                        dve.wait_ge(S["expd"], u + 1)
                        past(dve, S["att"], u - 3)
                        v.reciprocal(rden[:, q:q + 1], rsum[:, q:q + 1]).then_inc(S["rcp"], 1)
                        dve.wait_ge(S["pt_hi"], u + 1)
                        v.tensor_tensor(pt16[:, q % 2, 1, :, :],
                                        bank[:, 4 + q % 2, :].rearrange("p (k n) -> p k n", k=K),
                                        pt16[:, q % 2, 0, :, :], ALU.subtract).then_inc(S["pt_lo"], 1)
                        if q == 2 and within(b + 1, NB):
                            v_low(b + 1, 1 - p)
                        if isinstance(b, int) and b == 0:
                            stages[q]()
                in_pairs(dve, NB, body)

            def linear_attention():
                S = LIN
                st = S["step"]

                def front(b, i):
                    h = 2 * b + i
                    dve.wait_ge(S["sq_v"], 2 * h + 1)
                    norm2 = ss[:, i, 0, :]
                    v.tensor_reduce(norm2.rearrange("p (k h) -> p k h", k=KH),
                                    sq[:, i, :, :].rearrange("p k (h d) -> p k h d", d=DH), AX.X, ALU.add
                                    ).then_inc(st, 1)
                    dve.wait_ge(st, 4 * h + 1)
                    v.tensor_scalar(norm2, norm2, L2_EPS * L2_EPS, None, ALU.max).then_inc(st, 1)

                def normalise(b, i, p):
                    h = 2 * b + i
                    norm2, r, w = (ss[:, i, n, :] for n in range(3))
                    dve.wait_ge(S["r0"], 3 * h + 3)
                    v.scalar_tensor_tensor(out=w, in0=w, scalar=-0.5, in1=norm2, op0=ALU.mult,
                                           op1=ALU.mult).then_inc(st, 1)
                    dve.wait_ge(st, 4 * h + 3)
                    v.scalar_tensor_tensor(out=r, in0=w, scalar=1.5, in1=r, op0=ALU.add, op1=ALU.mult).then_inc(st, 1)
                    dve.wait_ge(st, 4 * h + 4)
                    dve.wait_ge(S["sq_v"], 2 * h + 2)
                    both = slice(KH * i, KH * i + KH)
                    v.tensor_tensor(qk_n[:, p, both, :].rearrange("p k (h d) -> p k h d", d=DH),
                                    bank[:, both, 0:2 * D].rearrange("p k (h d) -> p k h d", d=DH),
                                    r.rearrange("p (k h) -> p k h", k=KH).unsqueeze(3).to_broadcast(
                                        [P, KH, 2 * NH, DH]), ALU.mult).then_inc(S["qn"], 1)

                def state(b):
                    dve.wait_ge(S["kv"], b + 1)
                    rs = S["rstep"]
                    v.tensor_scalar(ks[:], bank[:, 4, D:D + 1], K_EPS, None, ALU.add).then_inc(rs, 1)
                    v.tensor_tensor(kvs[:, 0:D], bank[:, 4, 0:D], headmask[:], ALU.mult).then_inc(rs, 1)
                    dve.wait_ge(rs, 2 * b + 2)
                    v.tensor_scalar(kvs[:, D:D + NH], headcol[:], ks[:, 0:1], None, ALU.mult).then_inc(S["kvs"], 1)

                def result(b):
                    dve.wait_ge(S["out"], b + 1)
                    rd = S["rdn"]
                    o = bank[:, 6:8, 0:2 * (D + NH)].rearrange("p a (k n) -> p a k n", k=2)
                    v.reciprocal(rdn[:, :, :].rearrange("p (a k) h -> p a k h", a=2), o[:, :, :, D:D + NH]).then_inc(rd, 1)
                    dve.wait_ge(rd, b + 1)
                    dst = att(1, b)
                    for i in range(2):
                        both = slice(2 * i, 2 * i + 2)
                        ins = v.tensor_tensor(dst[:, both, :].rearrange("p k (h d) -> p k h d", d=DH),
                                              o[:, i, :, 0:D].rearrange("p k (h d) -> p k h d", d=DH),
                                              rdn[:, both, :].unsqueeze(3).to_broadcast([P, 2, NH, DH]), ALU.mult)
                    ins.then_inc(S["att"], 1)

                def body(b, j, p):
                    for i in range(2):
                        if within(b - 2, NB):
                            (state, result)[i](b - 2)
                        if within(b, NB):
                            normalise(b, i, p)
                        if i == 0 and within(b, NB):
                            front(b, 1)
                        if i == 1 and within(b + 1, NB):
                            front(b + 1, 0)
                        if isinstance(b, int) and b == 0:
                            stages[2 * i]()
                            stages[2 * i + 1]()
                counts, *stages = routing(1)
                choose(1, 1)
                counts()
                front(0, 0)
                in_pairs(dve, NB, body)
                body(NB, 0, 0)
                body(NB + 1, 0, 1)

            def experts(l):
                S = L[l]

                def step(s, j, r, e):
                    if within(s, MT):
                        dve.wait_ge(S["xg_t"], s + 1)
                        past(dve, S["up"], 2 * s - 2)
                        v.tensor_copy(xgt[:, r % 2, :, :],
                                      bank[:, r % 2, 0:TS].bitcast(F16).rearrange("p (h n) -> p h n", h=2)
                                      ).then_inc(S["xg_s"], 1)
                    if within(s - 1, MT):
                        u, ru = s - 1, (r + 1) % 2
                        past(dve, S["down"], u - 1)
                        for g in range(2):
                            hi, lo = (h16[:, ru, n, 2 * g:2 * g + 2, :].rearrange("p c n -> p (c n)") for n in range(2))
                            dve.wait_ge(S["h"], 4 * u + 2 * g + 2)
                            v.tensor_copy(hi, h32[:, g, :]).then_inc(S["h_hi"], 1)
                            dve.wait_ge(S["h_hi"], 2 * u + g + 1)
                            v.tensor_tensor(lo, h32[:, g, :], hi, ALU.subtract).then_inc(S["h_lo"], 1)
                    if within(s - 2, MT):
                        dve.wait_ge(S["down"], s - 1)
                        past(dve, S[f"st{r}"], 32 * j)
                        v.tensor_tensor(y_sb[:, r % 2, :, :],
                                        bank[:, 6 + r % 2, 0:2 * D].rearrange("p (t d) -> p t d", t=2),
                                        b2[:, l, e, :].to_broadcast([P, 2, D]), ALU.add).then_inc(S["y_v"], 1)
                    if within(s - 1, MT):
                        v.tensor_copy(ids[:, (r + 3) % 4, :].unsqueeze(2), xg[:, (r + 3) % 4, :, 2 * D:].bitcast(U32)
                                      ).then_inc(S["ids"], 1)
                if l == 0:
                    for zeroed in s_zeroed:
                        dve.wait_ge(zeroed, 16)
                dve.wait_ge(s_b2, 32)
                for s in range(2):
                    step(s, 0, s, None)
                e = experts_of(dve, 0, 6)
                for s in range(2, 8):
                    step(s, s // 4, s % 4, e[s - 2])
                with dve.Fori(1, MT // 8) as j:
                    e = experts_of(dve, 8 * j - 2, 8)
                    for r in range(8):
                        step(8 * j + r, 2 * j + r // 4, r % 4, e[r])
                last = MT // 8 * 8
                e = experts_of(dve, last - 2, MT - last + 2)
                for s in range(last, MT + 2):
                    step(s, s // 4, s % 4, e[s - last])

            def final():
                for u in range(NU):
                    if u + 1 in GATED:
                        dve.wait_ge(*y_in(u + 1))
                        y = y_last[u + 1]
                        v.tensor_tensor(y, y, unit(gate, u + 1).unsqueeze(2).to_broadcast([P, KU, D]),
                                        ALU.mult).then_inc(FIN["gated"], 1)
                    weigh(FIN, y_last[u], u, u % 2, 1)

            norm_stage(0)
            attention()
            experts(0)
            norm_stage(1)
            linear_attention()
            experts(1)
            final()

        @block.tensor
        def _(pe):
            def product(out, left, right, start=True, stop=True):
                pe.matmul(out, left(0), right(0), start=start, stop=False)
                pe.matmul(out, left(0), right(1), start=False, stop=False)
                return pe.matmul(out, left(1), right(0), start=False, stop=stop)

            pe.wait_ge(s_small, 16 * 10)
            pe.matmul(bank[:, 4, 0:D], wsmall[:, 0, :], wsmall[:, 1, :], start=True, stop=True).then_inc(s_prep_mm, 1)
            pe.wait_ge(s_const, 17)
            pe.transpose(bank[:, 5, 0:D], wsmall[:, 2, :], ident32[:]).then_inc(s_prep_mm, 1)
            for i in range(3):
                m = pe.transpose(bank[:, 6, i * D:i * D + D], wsmall[:, 3 + i, :], ident32[:])
            m.then_inc(s_prep_mm, 1)
            pe.transpose(bank[:, 7, 0:2 * E * C], b1_rows[:], ident32[0:2 * E * C, 0:2 * E * C]).then_inc(s_prep_mm, 1)

            def norm_stage(l):
                S = L[l]

                def turn(u, p):
                    pe.wait_ge(S["lo"], u + 1)
                    past(pe, S["xts"], u - 1)
                    hl = unit(xn16, u)
                    for i in range(2):
                        dst = bank[:, 2 * p + i, :].bitcast(F16).rearrange("p (h k n) -> p h k n", h=2, k=K)
                        for h in range(2):
                            for k in range(K):
                                m = pe.transpose(dst[:, h, k, :], hl[:, i * K + k, h, :], ident16[:])
                    m.then_inc(S["xt"], 1)

                def logits(u, p):
                    pe.wait_ge(S["xts"], u + 1)
                    past(pe, S["lg"], u - 1)
                    for i in range(2):
                        x = xnt(l, 2 * u + i)
                        for k in range(K):
                            n = (i * K + k) * E
                            m = product(bank[:, 4 + p, n:n + E], lambda h: x[:, h, k * P:k * P + P],
                                        lambda h: rw16[:, l, h, :])
                    m.then_inc(S["logits"], 1)

                def body(j):
                    if within(j - 1, NJ):
                        if l == 0 and j == 1:
                            pe.wait_ge(s_prep, 7)
                        for p in range(2):
                            logits(2 * j - 2 + p, p)
                    for p in range(2):
                        turn(2 * j + p, p)
                for j in range(NJ):
                    body(j)
                for p in range(2):
                    logits(NU - 2 + p, p)

            def ranks(l):
                pe.wait_ge(L[l]["onehot"], 2)
                oh = onehot[:].rearrange("p t e -> p (t e)")
                pe.matmul(bank[:, 6, :], before16[:], oh, start=True, stop=True)
                pe.matmul(bank[:, 5, :], ones16[:], oh, start=True, stop=True).then_inc(L[l]["rank"], 1)

            def attention():
                S = L[0]

                def t_of(b):
                    past(pe, S["v_lo"], b)
                    x = xnt(0, b)
                    product(bank[:, 7, :], lambda h: m16[:, h, :], lambda h: x[:, h, :]).then_inc(S["t_mm"], 1)

                def v_of(b):
                    pe.wait_ge(S["t_lo"], b + 1)
                    x = xnt(0, b)
                    for k in range(K):
                        m = product(bank[:, 7, k * D:k * D + D], lambda h: x[:, h, k * P:k * P + P],
                                    lambda h: wv16[:, h, :])
                    m.then_inc(S["v_mm"], 1)

                def scores(b, u, q, p):
                    pe.wait_ge(S["t_lo"], b + 1)
                    past(pe, S["expd"], u - 3)
                    x = xnt(0, b)
                    product(bank[:, q, :], lambda h: t16[:, p, h, q * P:q * P + P],
                            lambda h: x[:, h, :]).then_inc(S["score"], 1)

                def turn(u, q):
                    pe.wait_ge(S["expd"], u + 1)
                    past(pe, S["pt_lo"], u - 1)
                    for k in range(K):
                        m = pe.transpose(bank[:, 4 + q % 2, k * P:k * P + P], prob[:, q % 2, k * P:k * P + P],
                                         ident32[:])
                    m.then_inc(S["pt"], 1)

                def weigh(u, q, p):
                    pe.wait_ge(S["pt_lo"], u + 1)
                    past(pe, S["att"], u)
                    out = bank[:, 6, 0:D]
                    for k in range(K):
                        m = product(out, lambda h: pt16[:, q % 2, h, k, :], lambda h: v16[:, p, h, k, :],
                                    start=k == 0, stop=k == K - 1)
                    m.then_inc(S["pv"], 1)

                t_of(0)
                v_of(0)
                ranks(0)
                scores(0, 0, 0, 0)
                scores(0, 1, 1, 0)
                pe.wait_ge(S["routed"], 2)

                def body(b, j, p):
                    for q in range(K):
                        u = K * b + q
                        if q == 0 and within(b + 1, NB):
                            t_of(b + 1)
                        if within(u + 2, NT):
                            if q < 2:
                                scores(b, u + 2, q + 2, p)
                            else:
                                scores(b + 1, u + 2, q - 2, 1 - p)
                        turn(u, q)
                        if q == 2 and within(b + 1, NB):
                            v_of(b + 1)
                        if within(u - 1, NT):
                            weigh(u - 1, (q + 3) % K, p if q else 1 - p)
                in_pairs(pe, NB, body)
                weigh(NT - 1, K - 1, 1)

            def linear_attention():
                S = LIN

                def qkv(b, i):
                    past(pe, S["qn"], 2 * b + i - 1)
                    x = xnt(1, b)
                    for k in range(KH * i, KH * i + KH):
                        m = product(bank[:, k, 0:3 * D], lambda h: x[:, h, k * P:k * P + P],
                                    lambda h: wqkv16[:, h, :])
                    m.then_inc(S["qkv"], 1)

                def state(b, p):
                    pe.wait_ge(S["sp"], 2 * b + 2)
                    past(pe, S["kvs"], b)
                    for k in range(K):
                        m = pe.matmul(bank[:, 4, 0:D + 2], sp[:, p, k, D:2 * D], v_one[:, p, k, :],
                                      start=k == 0, stop=k == K - 1)
                    m.then_inc(S["kv"], 1)
                    past(pe, S["qts"], b)
                    for k in range(K):
                        m = pe.transpose(bank[:, 5, k * P:k * P + P], sp[:, p, k, 0:D], ident32[:])
                    m.then_inc(S["qt"], 1)

                def read(b):
                    pe.wait_ge(S["kvs"], b + 1)
                    pe.wait_ge(S["qts"], b + 1)
                    past(pe, S["att"], b)
                    for k in range(K):
                        n = (k % 2) * (D + NH)
                        m = pe.matmul(bank[:, 6 + k // 2, n:n + D + NH], q_t[:, k * P:k * P + P], kvs[:],
                                      start=True, stop=True)
                    m.then_inc(S["out"], 1)

                def body(b, j, p):
                    for i in range(2):
                        if i == 0 and within(b, NB):
                            qkv(b, 1)
                        if i == 1 and within(b + 1, NB):
                            qkv(b + 1, 0)
                        if i == 0 and within(b - 2, NB):
                            read(b - 2)
                        if i == 1 and within(b - 1, NB):
                            state(b - 1, 1 - p)
                qkv(0, 0)
                ranks(1)
                pe.wait_ge(L[1]["routed"], 2)
                in_pairs(pe, NB, body, peeled=2)
                body(NB, 0, 0)
                body(NB + 1, 0, 1)

            def experts(l):
                S = L[l]

                def turn(s, j, r):
                    pe.wait_ge(S[f"ld{r}"], 16 * (j + 1))
                    past(pe, S["xg_s"], s - 1)
                    dst = bank[:, r % 2, 0:TS].bitcast(F16).rearrange("p (h t n) -> p h t n", h=2, t=2)
                    for h in range(2):
                        for t in range(2):
                            m = pe.transpose(dst[:, h, t, :], xg[:, r, t, h * D:h * D + D], ident16[:])
                    m.then_inc(S["xg_t"], 1)

                def up(s, r, e):
                    pe.wait_ge(S["xg_s"], s + 1)
                    for g in range(2):
                        past(pe, S["h_lo"], 2 * s - 3 + g)
                        for c in range(2 * g, 2 * g + 2):
                            out = bank[:, 2 + 2 * (r % 2) + g, c % 2 * TS:c % 2 * TS + TS]
                            m = product(out, lambda h: w1_16[:, e, h, c * P:c * P + P], lambda h: xgt[:, r % 2, h, :])
                        m.then_inc(S["up"], 1)

                def down(s, r, e):
                    pe.wait_ge(S["h_lo"], 2 * s + 2)
                    past(pe, S["y_v"], s - 1)
                    for t in range(2):
                        out = bank[:, 6 + r % 2, t * D:t * D + D]
                        for c in range(C):
                            m = product(out, lambda h: h16[:, r % 2, h, c, t * P:t * P + P],
                                        lambda h: w2_16[:, e, h, c, :], start=c == 0, stop=c == C - 1)
                    m.then_inc(S["down"], 1)

                def step(s, j, r, e, at):
                    if within(s, MT):
                        turn(s, j, r)
                    if within(s - 1, MT):
                        up(s - 1, r + 1, e[at + 1])
                    if within(s - 2, MT):
                        down(s - 2, r, e[at])

                pe.wait_ge(S["routed"], 4)
                for part in ("w1_lo", "w2_lo"):
                    pe.wait_ge(S[part], E)
                e = experts_of(pe, 0, 7)
                for s in range(8):
                    step(s, s // 4, s % 4, e, s - 2)
                with pe.Fori(1, MT // 8) as j:
                    e = experts_of(pe, 8 * j - 2, 9)
                    for r in range(8):
                        step(8 * j + r, 2 * j + r // 4, r % 4, e, r)
                last = MT // 8 * 8
                e = experts_of(pe, last - 2, MT - last + 2)
                for s in range(last, MT + 2):
                    step(s, s // 4, s % 4, e, s - last)

            norm_stage(0)
            attention()
            experts(0)
            norm_stage(1)
            linear_attention()
            experts(1)


_INS = ['L0_attn_x', 'L0_attn_Wq', 'L0_attn_Wk', 'L0_attn_Wv', 'L0_ffn_gate_w', 'L0_ffn_gate_b', 'L0_ffn_w1',
        'L0_ffn_b1', 'L0_ffn_w2', 'L0_ffn_b2', 'L1_attn_W_qkv', 'L1_ffn_router_W', 'L1_ffn_router_b', 'L1_ffn_W1',
        'L1_ffn_b1', 'L1_ffn_W2', 'L1_ffn_b2']


def kernel(**inputs):
    import numpy as _np
    import concourse.bacc as _bacc
    from concourse import mybir as _mybir
    from concourse.bass_utils import run_bass_kernel_spmd as _run

    nc = _bacc.Bacc("TRN2", target_bir_lowering=False, num_devices=1)
    arrays, args = {}, []
    for name in _INS:
        a = _np.ascontiguousarray(inputs[name])
        arrays[f"in_{name}"] = a
        args.append(nc.dram_tensor(f"in_{name}", a.shape, _mybir.dt.from_np(a.dtype), kind="ExternalInput").ap())
    shape = inputs['L0_attn_x'].shape
    args.append(nc.dram_tensor("out", shape, _mybir.dt.float32, kind="ExternalOutput").ap())
    build(nc, *args)
    r = _run(nc, [arrays], core_ids=[0])
    return r.results[0]["out"]
```
